# Optimizing a Trainium2 kernel written in Bass

```python
import numpy as np
import jax
import jax.numpy as jnp

def _softmax(x, axis=-1):
    return jax.nn.softmax(x, axis=axis)

def _gelu(x):
    return jax.nn.gelu(x, approximate=True)

def _silu(x):
    return jax.nn.silu(x)

def _sigmoid(x):
    return jax.nn.sigmoid(x)

def _layernorm(x, axis=-1, eps=1e-05):
    m = jnp.mean(x, axis=axis, keepdims=True)
    v = jnp.var(x, axis=axis, keepdims=True)
    return (x - m) / jnp.sqrt(v + eps)

def _scatter_add(tgt, idx, src, axis=0):
    return tgt.at[idx].add(src)

def _segment_sum(src, seg, n):
    return jax.ops.segment_sum(src, seg, n)
kernel_name = 'mk_flamingo_gated_d2_seqx_r4_74d05b'

def setup_inputs(seed: int=0):
    np.random.seed(seed)
    _w = jnp.asarray

    def _rec_inputs():
        import jax
        import jax.numpy as jnp
        _rk = jax.random.key(seed)
        x = -0.0003929 + 0.9999 * jax.random.normal(jax.random.fold_in(_rk, 1), (8, 256, 256), jnp.float32)
        _lenS = 256 - jax.random.randint(jax.random.fold_in(_rk, 7), (8,), 0, max(1, 256 // 4) + 1, jnp.int32)
        _lenS2 = 120 - jax.random.randint(jax.random.fold_in(_rk, 8), (8,), 0, max(1, 120 // 4) + 1, jnp.int32)
        _ctx_512P = jax.random.normal(jax.random.fold_in(_rk, 11), (8, 16, 128), jnp.float32)
        _ctx_512c = jax.random.dirichlet(jax.random.fold_in(_rk, 511), 0.3 * jnp.ones((16,), jnp.float32), (8, 120))
        _ctx_512t = jnp.einsum('bsk,bkd->bsd', _ctx_512c, _ctx_512P)
        _ctx_512t = _ctx_512t * jax.lax.rsqrt(jnp.mean(jnp.square(_ctx_512t)) + 1e-12) * 0.953939
        ctx_512 = 4.13588e-05 + 0.999923 * (_ctx_512t + 0.3 * jax.random.normal(jax.random.fold_in(_rk, 611), (8, 120, 128), jnp.float32))
        _g = jax.random.normal(jax.random.fold_in(_rk, 9001), (2, 2), jnp.float32)
        _g = jnp.sign(_g) * jnp.maximum(jnp.abs(_g), 1.0) + (_g == 0) * 1.0
        g_xattn = _g[0]
        g_ffn = _g[1]
        return (x, ctx_512, g_xattn, g_ffn)
    x, ctx_512, g_xattn, g_ffn = _rec_inputs()

    def _L0_xattn_setup():
        import jax, jax.numpy as jnp
        import numpy as np
        B, LQ, LK = (8, 512, 512)
        QD, KD, VD = (256, 128, 128)
        key = jax.random.key(seed)
        ks = jax.random.split(key, 9)
        s = 0.02
        return {'query': jax.random.normal(ks[0], (B, LQ, QD), jnp.float32), 'key': jax.random.normal(ks[1], (B, LK, KD), jnp.float32), 'value': jax.random.normal(ks[2], (B, LK, VD), jnp.float32), 'Wq': jax.random.normal(ks[3], (QD, QD), jnp.float32) * s, 'bq': jnp.zeros((QD,), jnp.float32), 'Wk': jax.random.normal(ks[4], (KD, QD), jnp.float32) * s, 'bk': jnp.zeros((QD,), jnp.float32), 'Wv': jax.random.normal(ks[5], (VD, QD), jnp.float32) * s, 'bv': jnp.zeros((QD,), jnp.float32)}
    _L0_xattn_all = _L0_xattn_setup()
    _L0_xattn_in = {k: v for k, v in _L0_xattn_all.items() if k in ('Wq', 'bq', 'Wk', 'bk', 'Wv', 'bv')}
    del _L0_xattn_all

    def _L0_ffn_setup():
        import jax, jax.numpy as jnp
        import numpy as np
        B, S, D = (2, 512, 256)
        DFF = 512
        E_FFN = 8
        E_ZERO = 4
        E_TOT = E_FFN + E_ZERO
        TOP_K = 2
        key = jax.random.key(seed)
        k1, k2, k3, k4 = jax.random.split(key, 4)
        x = jax.random.normal(k1, (B, S, D), dtype=jnp.float32)
        gate_w = jax.random.normal(k2, (E_TOT, D), dtype=jnp.float32) * (1.0 / np.sqrt(D))
        expert_bias = jnp.zeros((E_TOT,), dtype=jnp.float32)
        w1 = jax.random.normal(k3, (E_FFN, DFF, D), dtype=jnp.float32) * (1.0 / np.sqrt(D))
        w2 = jax.random.normal(k4, (E_FFN, D, DFF), dtype=jnp.float32) * (1.0 / np.sqrt(DFF))
        return {'x': x, 'gate_w': gate_w, 'expert_bias': expert_bias, 'w1': w1, 'w2': w2}
    _L0_ffn_all = _L0_ffn_setup()
    _L0_ffn_in = {k: v for k, v in _L0_ffn_all.items() if k in ('gate_w', 'expert_bias', 'w1', 'w2')}
    del _L0_ffn_all

    def _L1_xattn_setup():
        import jax, jax.numpy as jnp
        import numpy as np
        HEADS = 16
        D_MODEL = 256
        IMG_MODEL = 128
        D_K = D_MODEL // HEADS
        key = jax.random.key(seed)
        ks = jax.random.split(key, 12)
        B, LQ, LKV = (8, 512, 256)
        s_dm = 1.0 / np.sqrt(D_MODEL)
        s_im = 1.0 / np.sqrt(IMG_MODEL)
        return {'q': jax.random.normal(ks[0], (B, LQ, D_MODEL), jnp.float32), 'k': jax.random.normal(ks[1], (B, LKV, IMG_MODEL), jnp.float32), 'v': jax.random.normal(ks[2], (B, LKV, IMG_MODEL), jnp.float32), 'Wq': jax.random.normal(ks[3], (D_MODEL, D_MODEL), jnp.float32) * s_dm, 'bq': jnp.zeros((D_MODEL,), jnp.float32), 'Wk': jax.random.normal(ks[4], (IMG_MODEL, D_MODEL), jnp.float32) * s_im, 'bk': jnp.zeros((D_MODEL,), jnp.float32), 'Wv': jax.random.normal(ks[5], (IMG_MODEL, D_MODEL), jnp.float32) * s_im, 'bv': jnp.zeros((D_MODEL,), jnp.float32), 'Wo': jax.random.normal(ks[6], (D_MODEL, D_MODEL), jnp.float32) * s_dm, 'bo': jnp.zeros((D_MODEL,), jnp.float32)}
    _L1_xattn_all = _L1_xattn_setup()
    _L1_xattn_in = {k: v for k, v in _L1_xattn_all.items() if k in ('Wq', 'bq', 'Wk', 'bk', 'Wv', 'bv', 'Wo', 'bo')}
    del _L1_xattn_all

    def _L1_ffn_setup():
        import jax, jax.numpy as jnp
        import numpy as np
        FP8_MAX = 448.0

        def quant_fp8(x):
            amax = jnp.max(jnp.abs(x)).astype(jnp.float32)
            scale = jnp.minimum(FP8_MAX / jnp.maximum(amax, 1e-12), FP8_MAX)
            x_fp8 = jnp.clip(x * scale, -FP8_MAX, FP8_MAX).astype(jnp.float8_e4m3fn)
            return (x_fp8, 1.0 / scale)
        key = jax.random.key(seed)
        k1, k2, k3 = jax.random.split(key, 3)
        B, S, IN, OUT = (4, 2048, 256, 256)
        input = jax.random.normal(k1, (B, S, IN), dtype=jnp.float32)
        bound = 1.0 / np.sqrt(IN)
        weight = jax.random.uniform(k2, (OUT, IN), dtype=jnp.float32, minval=-bound, maxval=bound)
        bias = jax.random.uniform(k3, (OUT,), dtype=jnp.float32, minval=-bound, maxval=bound)
        return {'input': input, 'weight': weight, 'bias': bias}
    _L1_ffn_all = _L1_ffn_setup()
    _L1_ffn_in = {k: v for k, v in _L1_ffn_all.items() if k in ('weight', 'bias')}
    del _L1_ffn_all
    return {'x': x, 'ctx_512': ctx_512, 'g_xattn': g_xattn, 'g_ffn': g_ffn, 'L0_xattn_Wq': _L0_xattn_in['Wq'], 'L0_xattn_bq': _L0_xattn_in['bq'], 'L0_xattn_Wk': _L0_xattn_in['Wk'], 'L0_xattn_bk': _L0_xattn_in['bk'], 'L0_xattn_Wv': _L0_xattn_in['Wv'], 'L0_xattn_bv': _L0_xattn_in['bv'], 'L0_ffn_gate_w': _L0_ffn_in['gate_w'], 'L0_ffn_expert_bias': _L0_ffn_in['expert_bias'], 'L0_ffn_w1': _L0_ffn_in['w1'], 'L0_ffn_w2': _L0_ffn_in['w2'], 'L1_xattn_Wq': _L1_xattn_in['Wq'], 'L1_xattn_bq': _L1_xattn_in['bq'], 'L1_xattn_Wk': _L1_xattn_in['Wk'], 'L1_xattn_bk': _L1_xattn_in['bk'], 'L1_xattn_Wv': _L1_xattn_in['Wv'], 'L1_xattn_bv': _L1_xattn_in['bv'], 'L1_xattn_Wo': _L1_xattn_in['Wo'], 'L1_xattn_bo': _L1_xattn_in['bo'], 'L1_ffn_weight': _L1_ffn_in['weight'], 'L1_ffn_bias': _L1_ffn_in['bias']}

def reference(x, ctx_512, g_xattn, g_ffn, L0_xattn_Wq, L0_xattn_bq, L0_xattn_Wk, L0_xattn_bk, L0_xattn_Wv, L0_xattn_bv, L0_ffn_gate_w, L0_ffn_expert_bias, L0_ffn_w1, L0_ffn_w2, L1_xattn_Wq, L1_xattn_bq, L1_xattn_Wk, L1_xattn_bk, L1_xattn_Wv, L1_xattn_bv, L1_xattn_Wo, L1_xattn_bo, L1_ffn_weight, L1_ffn_bias):
    import jax
    import jax.numpy as jnp

    def _L0_xattn_ref(query, key, value, Wq, bq, Wk, bk, Wv, bv):
        import jax, jax.numpy as jnp
        import numpy as np
        B, LQ, LK = (8, 512, 512)
        QD, KD, VD = (256, 128, 128)
        q = jnp.einsum('bld,de->ble', query, Wq) + bq
        k = jnp.einsum('bld,de->ble', key, Wk) + bk
        v = jnp.einsum('bld,de->ble', value, Wv) + bv
        scores = jnp.einsum('bqe,bke->bqk', q, k)
        attn = jax.nn.softmax(scores, axis=-1)
        out = jnp.einsum('bqk,bke->bqe', attn, v)
        return out

    def _L0_ffn_ref(x, gate_w, expert_bias, w1, w2):
        import jax, jax.numpy as jnp
        import numpy as np
        B, S, D = (2, 512, 256)
        DFF = 512
        E_FFN = 8
        E_ZERO = 4
        E_TOT = E_FFN + E_ZERO
        TOP_K = 2
        logits = jnp.einsum('btd,ed->bte', x, gate_w) + expert_bias
        topk_logits, topk_idx = jax.lax.top_k(logits, TOP_K)
        topk_w = jax.nn.softmax(topk_logits, axis=-1)
        onehot = jax.nn.one_hot(topk_idx, E_TOT, dtype=x.dtype)
        w = jnp.einsum('btk,btke->bte', topk_w, onehot)
        w_ffn = w[..., :E_FFN]
        w_zero = jnp.sum(w[..., E_FFN:], axis=-1)
        h = jax.nn.silu(jnp.einsum('btd,efd->btef', x, w1))
        y = jnp.einsum('btef,edf->bted', h, w2)
        out = jnp.einsum('bte,bted->btd', w_ffn, y) + w_zero[..., None] * x
        return out

    def _L1_xattn_ref(q, k, v, Wq, bq, Wk, bk, Wv, bv, Wo, bo):
        import jax, jax.numpy as jnp
        import numpy as np
        HEADS = 16
        D_MODEL = 256
        IMG_MODEL = 128
        D_K = D_MODEL // HEADS
        B, LQ, _ = q.shape
        LKV = k.shape[1]
        qh = (q @ Wq + bq).reshape(B, LQ, HEADS, D_K).transpose(0, 2, 1, 3)
        kh = (k @ Wk + bk).reshape(B, LKV, HEADS, D_K).transpose(0, 2, 1, 3)
        vh = (v @ Wv + bv).reshape(B, LKV, HEADS, D_K).transpose(0, 2, 1, 3)
        scale = 1.0 / np.sqrt(D_K)
        scores = jnp.einsum('bhqd,bhkd->bhqk', qh, kh) * scale
        attn = jax.nn.softmax(scores, axis=-1)
        out = jnp.einsum('bhqk,bhkd->bhqd', attn, vh)
        concat = out.transpose(0, 2, 1, 3).reshape(B, LQ, D_MODEL)
        return concat @ Wo + bo

    def _L1_ffn_ref(input, weight, bias):
        import jax, jax.numpy as jnp
        import numpy as np
        FP8_MAX = 448.0

        def quant_fp8(x):
            amax = jnp.max(jnp.abs(x)).astype(jnp.float32)
            scale = jnp.minimum(FP8_MAX / jnp.maximum(amax, 1e-12), FP8_MAX)
            x_fp8 = jnp.clip(x * scale, -FP8_MAX, FP8_MAX).astype(jnp.float8_e4m3fn)
            return (x_fp8, 1.0 / scale)
        prev_shape = input.shape
        x2d = input.reshape(-1, weight.shape[1])
        w_fp8, w_scale = quant_fp8(weight)
        x_fp8, x_scale = quant_fp8(x2d)
        acc = jnp.matmul(x_fp8.astype(jnp.float32), w_fp8.astype(jnp.float32).T)
        out2d = (acc * (x_scale * w_scale) + bias).astype(jnp.bfloat16)
        out = out2d.reshape(*prev_shape[:-1], weight.shape[0]).astype(input.dtype)
        return out
    x = x + jnp.tanh(g_xattn[0]) * _L0_xattn_ref(_layernorm(x, axis=-1), ctx_512, ctx_512, L0_xattn_Wq, L0_xattn_bq, L0_xattn_Wk, L0_xattn_bk, L0_xattn_Wv, L0_xattn_bv)
    x = x + jnp.tanh(g_ffn[0]) * _L0_ffn_ref(_layernorm(x, axis=-1), L0_ffn_gate_w, L0_ffn_expert_bias, L0_ffn_w1, L0_ffn_w2)
    x = x + jnp.tanh(g_xattn[1]) * _L1_xattn_ref(_layernorm(x, axis=-1), ctx_512, ctx_512, L1_xattn_Wq, L1_xattn_bq, L1_xattn_Wk, L1_xattn_bk, L1_xattn_Wv, L1_xattn_bv, L1_xattn_Wo, L1_xattn_bo)
    x = x + jnp.tanh(g_ffn[1]) * _L1_ffn_ref(_layernorm(x, axis=-1), L1_ffn_weight, L1_ffn_bias)
    return x

_drawn_inputs = setup_inputs


def setup_inputs(seed=0):
    import zlib

    import numpy as np

    out = dict(_drawn_inputs(seed))
    spreads = {'g_ffn': (-1.0, 0.2),
     'L0_xattn_bq': (0.0, 0.1),
     'L0_xattn_bk': (0.0, 0.8),
     'L0_xattn_bv': (0.0, 0.1),
     'L0_ffn_expert_bias': (0.0, 0.1),
     'L1_xattn_bq': (0.0, 0.315),
     'L1_xattn_bk': (0.0, 0.8),
     'L1_xattn_bv': (0.0, 0.1),
     'L1_xattn_bo': (0.0, 0.1)}
    factors = {}
    for name, (base, spread) in spreads.items():
        noise = np.random.default_rng([zlib.crc32(name.encode()), seed]).standard_normal(out[name].shape)
        drawn = base * np.exp(spread * noise) if base else spread * noise
        out[name] = jnp.asarray(drawn.astype(out[name].dtype))
    for name, factor in factors.items():
        out[name] = (out[name] * factor).astype(out[name].dtype)
    return out
```

```python
from contextlib import ExitStack

import concourse.bass as bass
import numpy as np
from concourse import mybir

ALU = mybir.AluOpType
ACT = mybir.ActivationFunctionType
AX = mybir.AxisListType.X
F32, F32R, BF16, F16, I32 = (mybir.dt.float32, mybir.dt.float32r, mybir.dt.bfloat16, mybir.dt.float16,
                             mybir.dt.int32)

P = 128
B, S, D = 8, 256, 256
LK = 120
U = S // P
TILES = B * U
C = D // P
E_ALL, E_FFN, FF = 12, 8, 512
FC = FF // P
WE = C * FF + FC * D
CHUNK = 512
CHUNKS = E_FFN * WE // CHUNK
BLOCKS = 2 * TILES + E_FFN
HEADS, DK = 16, 16
HV = DK + 1
NB = 4
HG = HEADS // NB
EPS = 1e-5
FP8_MAX = 448.0
MAGIC = 1.5 * 2.0 ** 20
TINY = 2.0 ** -6


class Chain:

    def __init__(self, eng, sem, tick):
        self.eng, self.sem, self.tick, self.n, self.seen = eng, sem, tick, 0, 0

    def mark(self, ins):
        ins.then_inc(self.sem, 1)
        self.n = self.n + 1
        self.seen += 1

    def settle(self):
        self.eng.wait_ge(self.sem, self.n)

    def settle_apart(self):
        wait_apart(self.eng, self.sem, self.n, self.tick)

    def loop(self, first, last, per, body):
        base = self.n
        with self.eng.Fori(first, last) as i:
            self.n, self.seen = i * per + (base - first * per), 0
            body(i)
            assert self.seen == per, (self.seen, per)
        self.n = base + per * (last - first)


def wait(eng, sem, value):
    if not isinstance(value, int) or value > 0:
        eng.wait_ge(sem, value)


def wait_apart(eng, sem, value, tick):
    wait(eng, sem, value)
    if not isinstance(value, int):
        eng.sem_inc(tick, 1)


def cols(i, n):
    return slice(i * n, i * n + n) if isinstance(i, int) else bass.ds(i * n, n)


def build(nc, x, ctxT, wq0T, wk0, wv0, bq0, bk0, bv0, gateT, gbias, wmoe, wq1, wk1, wv1, wo1,
          bq1, bk1, bv1, bo1, wfT, bf, gains, c_ident, c_tri, c_count, c_token, c_head, out):
    ctx = ExitStack()
    with ctx:
        def sb(name, shape, dt=F32, stack=ctx):
            return stack.enter_context(nc.sbuf_tensor(name, shape, dt))

        def sem(name):
            return ctx.enter_context(nc.semaphore(name))

        bank = [ctx.enter_context(nc.psum_tensor(f"bank{i}", [P, 512], F32)) for i in range(8)]
        xn_d = nc.dram_tensor("xn_d", [B * S, D], F32).ap()
        y_d = nc.dram_tensor("y_d", [BLOCKS * P, D], F32).ap()

        x_sb = sb("x_sb", [P, TILES * D])
        ident = sb("ident", [P, P])
        identb = sb("identb", [P, P], BF16)
        gains_sb = sb("gains_sb", [P, 4])
        gain = sb("gain", [P, 4])
        ones = sb("ones", [2, P])
        half = sb("half", [P, U])
        cw = sb("cw", [P, 2 * TILES])
        cz = sb("cz", [P, TILES])
        pos_i = sb("pos_i", [P, 2 * TILES], I32)
        slot_i = sb("slot_i", [P, BLOCKS], I32)
        blk_i = sb("blk_i", [P, BLOCKS], I32)
        pos_now = sb("pos_now", [P, 4], I32)
        slot_now = sb("slot_now", [P, 2], I32)
        stat = sb("stat", [P, U, 6])
        mean = sb("mean", [P, U, 2])
        var = sb("var", [P, U])
        rstd = sb("rstd", [P, U])
        stat1 = sb("stat1", [P, U, 6])
        mean1 = sb("mean1", [P, U, 2])
        var1 = sb("var1", [P, U])
        rstd1 = sb("rstd1", [P, U])
        bk1_sb = sb("bk1_sb", [P, C])
        kmask = sb("kmask", [P, 2])
        kv = ExitStack()
        kq = sb("kq", [P, B * C * LK], F32, kv)
        v0 = sb("v0", [LK, B * D], F32, kv)
        bqk = sb("bqk", [1, B * LK], F32, kv)
        kv.close()
        kt1 = sb("kt1", [P, C * B * LK])
        v1 = sb("v1", [LK, B * HEADS * HV])
        fill = sb("fill", [P, (C * B * LK + B * D + B * LK) - (C * B * LK + B * HEADS * HV)])
        moe = ExitStack()
        wh = sb("wh", [P, E_FFN * WE], F32R, moe)
        wl = sb("wl", [P, E_FFN * WE], F32R, moe)
        con = ExitStack()
        ctxT_sb = sb("ctxT_sb", [P, B * LK], F32, con)
        wk1_sb = sb("wk1_sb", [P, D], F32, con)
        wv1_sb = sb("wv1_sb", [P, D], F32, con)
        bv1_sb = sb("bv1_sb", [P, D], F32, con)
        tri = sb("tri", [P, 2 * P], BF16, con)
        count = sb("count", [P, P], F32, con)
        token = sb("token", [P, 2 * TILES], F32, con)
        logit = sb("logit", [P, TILES * E_ALL], F32, con)
        att = ExitStack()
        wq0_sb = sb("wq0_sb", [P, C, D], F32, att)
        wk0_sb = sb("wk0_sb", [P, D], F32, att)
        wv0_sb = sb("wv0_sb", [P, D], F32, att)
        bq0_sb = sb("bq0_sb", [P, C], F32, att)
        bk0_sb = sb("bk0_sb", [P, C], F32, att)
        bv0_sb = sb("bv0_sb", [P, D], F32, att)
        gate_sb = sb("gate_sb", [P, C, E_ALL], F32, att)
        gbias_sb = sb("gbias_sb", [P, U * E_ALL], F32, att)
        negmax = sb("negmax", [P, U], F32, att)
        psum = sb("psum", [P, U], F32, att)
        rsum = sb("rsum", [P, U], F32, att)
        rsumg = sb("rsumg", [P, U], F32, att)
        stage = sb("stage", [P, 2, CHUNK], F32, att)
        xq = sb("xq", [P, U * D], F32, att)
        early = ExitStack()
        kt0 = sb("kt0", [P, C, B * LK], F32, early)
        early.close()
        xT = sb("xT", [P, C * S], F32, att)
        prob = sb("prob", [P, U * LK], F32, att)
        probT = sb("probT", [LK, S], F32, att)
        xq1 = sb("xq1", [P, U * D], F32, att)
        xT1 = sb("xT1", [P, C * S], F32, att)
        att.close()
        rt = ExitStack()
        V3 = [P, TILES, E_ALL]
        eq = sb("eq", V3, F32, rt)
        cand = sb("cand", V3, F32, rt)
        left = sb("left", V3, F32, rt)
        hot = sb("hot", [P, 2, TILES, E_ALL], F32, rt)
        top = sb("top", [P, 2, TILES], F32, rt)
        pick = sb("pick", [P, TILES], F32, rt)
        dif = sb("dif", [P, TILES], F32, rt)
        ex = sb("ex", [P, TILES], F32, rt)
        wgt = sb("wgt", [P, 2, TILES], F32, rt)
        valid = sb("valid", [P, 2, TILES], F32, rt)
        wval = sb("wval", [P, 2, TILES], F32, rt)
        pairs = sb("pairs", [P, TILES, E_FFN], BF16, rt)
        pad = TILES // 2
        pre = [sb(f"pre{i}", [P, pad + TILES, E_FFN], F32, rt) for i in range(2)]
        cnt_i = sb("cnt_i", [P, E_FFN], I32, rt)
        nb_i = sb("nb_i", [P, E_FFN], I32, rt)
        nb = [sb(f"nb{i}", [P, 4 + E_FFN], F32, rt) for i in range(2)]
        nbk = sb("nbk", [P, E_FFN], F32, rt)
        place = sb("place", [P, TILES, E_FFN], F32, rt)
        prod = sb("prod", [P, 2, TILES, E_FFN], F32, rt)
        pos = sb("pos", [P, 2 * TILES], F32, rt)
        row_i = sb("row_i", [P, 2 * TILES], I32, rt)
        col_i = sb("col_i", [P, 2 * TILES], I32, rt)
        row = sb("row", [P, 2 * TILES], F32, rt)
        col = sb("col", [P, 2 * TILES], F32, rt)
        onerow = sb("onerow", [P, 2, 8, P], F16, rt)
        onecol = sb("onecol", [P, 2 * TILES, BLOCKS], F16, rt)
        tokcol = sb("tokcol", [P, 2 * TILES, BLOCKS], F16, rt)
        cmp = sb("cmp", [P, BLOCKS, E_FFN - 1], F32, rt)
        blk = sb("blk", [P, BLOCKS], F32, rt)
        rt.close()
        con.close()
        ex_ = ExitStack()
        xg = sb("xg", [P, 2, D], F32, ex_)
        xh = sb("xh", [P, 2, D], F32R, ex_)
        xl = sb("xl", [P, 2, D], F32R, ex_)
        th = sb("th", [P, FF], F32, ex_)
        gate = sb("gate", [P, 2, FF], F32, ex_)
        gh = sb("gh", [P, 2, FF], F32R, ex_)
        gl = sb("gl", [P, 2, FF], F32R, ex_)
        y_sb = sb("y_sb", [P, 2, D], F32, ex_)
        xz = sb("xz", [P, U * D], F32, ex_)
        ex_.close()
        moe.close()
        xn_sb = sb("xn_sb", [P, TILES * D])
        wq1_sb = sb("wq1_sb", [P, C, D])
        wo1_sb = sb("wo1_sb", [P, C, D])
        bq1_sb = sb("bq1_sb", [P, C])
        bo1_sb = sb("bo1_sb", [P, D])
        bo1g = sb("bo1g", [P, D])
        bf_sb = sb("bf_sb", [P, D])
        wf_sb = sb("wf_sb", [P, C * D])
        wf8 = sb("wf8", [P, C * D], BF16)
        know = sb("know", [P, 2, C * LK])
        yg = sb("yg", [P, 4, D])
        xq2 = sb("xq2", [P, 2, D])
        xT2 = sb("xT2", [P, D])
        qT = sb("qT", [P, D])
        nm = sb("nm", [P, HEADS])
        sc = sb("sc", [P, NB, HG * LK])
        pT = sb("pT", [LK, NB, HG * P])
        rec = sb("rec", [P, HEADS])
        o_sb = sb("o_sb", [P, D])
        oT = sb("oT", [P, D])
        amx = sb("amx", [P, TILES])
        red = sb("red", [P, 16])
        yq = sb("yq", [P, 2 * D])
        ye = sb("ye", [P, 2 * D], I32)
        ym = sb("ym", [P, 2 * D])
        yt = sb("yt", [P, 2 * D])
        y8 = sb("y8", [P, 2 * D], BF16)
        y8T = sb("y8T", [P, C * S], BF16)
        zf = sb("zf", [P, 2, 2 * D], BF16)
        of = sb("of", [P, 2, 2 * D])
        peak = sb("peak", [2, 1])
        peaks = sb("peaks", [2, 2])


        x0_in, x_in, con_in, att_in, cst_in, l1_in = map(sem, "x0_in x_in con_in att_in cst_in l1_in".split())
        set_up, gain_ok = map(sem, "set_up gain_ok".split())
        pe_tick, act_tick, dve_tick, pool_tick = map(sem, "pe_tick act_tick dve_tick pool_tick".split())
        pe_own, act_own, dve_own, pool_own = map(sem, "pe_own act_own dve_own pool_own".split())
        p0_mm, p0_act, p0_dve = map(sem, "p0_mm p0_act p0_dve".split())
        (xq_ready, xT_done, xT_copied, scores_done, max_done, exp_done, probT_done, probT_copied, pv_done, x1_done,
         xq1_ready, xT1_done, xT1_copied, logit_done, logit_kept, var_ok, rstd_ok, var1_ok, rstd1_ok) = map(sem, (
            "xq_ready xT_done xT_copied scores_done max_done exp_done probT_done probT_copied pv_done x1_done "
            "xq1_ready xT1_done xT1_copied logit_done logit_kept var_ok rstd_ok var1_ok rstd1_ok").split())
        xn_stored = sem("xn_stored")
        chunk_in = [sem(f"chunk_in{k}") for k in range(2)]
        split_h, split_l = map(sem, "split_h split_l".split())

        (pairs_ok, rank_done, dif_ok, ex_ok, tok_ok, onerow_ok, onerow_used, slots_done, slots_kept, blocks_kept,
         pos_kept, cw_ok, cz_ok, ones_ok) = map(sem, (
            "pairs_ok rank_done dif_ok ex_ok tok_ok onerow_ok onerow_used slots_done slots_kept blocks_kept "
            "pos_kept cw_ok cz_ok ones_ok").split())
        gathered = [sem(f"gathered{k}") for k in range(2)]
        y_stored = [sem(f"y_stored{k}") for k in range(2)]
        xz_in, xz_used = sem("xz_in"), sem("xz_used")
        (xgT_done, xh_ok, xl_ok, h_done, th_ok, gate_ok, g_done, gh_ok, gl_ok, y_done, y_kept) = map(sem, (
            "xgT_done xh_ok xl_ok h_done th_ok gate_ok g_done gh_ok gl_ok y_done y_kept").split())

        y_here = [sem(f"y_here{k}") for k in range(2)]
        (x2_ok, l2_var, l2_rstd, xn2_ok, l3_var, l3_rstd, know_ok, bo_ok, bo_added, s_done, sub_ok, e_ok, t_done,
         pT_ok, pvj_done, xt_done, xt_ok, q_done, q_ok, on_ok, ot_done, ot_ok, wo_done, x3_ok, amax_ok) = map(sem, (
            "x2_ok l2_var l2_rstd xn2_ok l3_var l3_rstd know_ok bo_ok bo_added s_done sub_ok e_ok t_done "
            "pT_ok pvj_done xt_done xt_ok q_done q_ok on_ok ot_done ot_ok wo_done x3_ok amax_ok").split())
        (red_ok, red_done, peak_ok, peak_done, wf8_ok, y8_ok, y8_done, y8T_ok, acc_done, acc_used, of_ok) = map(sem, (
            "red_ok red_done peak_ok peak_done wf8_ok y8_ok y8_done y8T_ok acc_done acc_used of_ok").split())
        stored = [sem(f"stored{k}") for k in range(2)]

        def ahead_of(i, k, n):
            return i + (k + n) // 2, (k + n) % 2

        IN_CON, IN_ATT, IN_CST = 16 * 4, 16 * 9, 16 * 6

        block = ctx.enter_context(nc.Block())

        P0 = [("kt0", m, h) for m in range(C) for h in range(2)] + [("kq", m, h) for m in range(C) for h in range(2)] \
            + [("bqk", 0, h) for h in range(2)] + [("v0", b, 0) for b in range(B)]
        P1 = [("kt1", m, h) for m in range(C) for h in range(2)] + [("v1", b, 0) for b in range(B)]
        BY = {"kt0": "act", "kq": "dve", "bqk": "act", "v0": "dve", "kt1": "act", "v1": "act"}
        HB = B // 2 * LK

        def evacuated(n):
            items = P0 + P1
            who = BY[items[n][0]]
            return who, sum(BY[it[0]] == who for it in items[:n + 1])

        def p0_bank(n):
            return bank[4 + n % 4]

        @block.sync
        def _(sp):
            xv = x.rearrange("(b p u) n -> p b (u n)", p=P, u=U)
            x4 = x_sb[:].rearrange("p (b n) -> p b n", b=B)
            sp.dma_start(x4[:, 0:1, :], xv[:, 0:1, :]).then_inc(x0_in, 16)
            sp.dma_start(ctxT_sb[:], ctxT).then_inc(att_in, 16)
            for dst, src in ((wk0_sb, wk0), (bk0_sb, bk0), (wq0_sb, wq0T), (bq0_sb, bq0), (wv0_sb, wv0)):
                sp.dma_start(dst[:], src).then_inc(att_in, 16)
            sp.dma_start(bv0_sb[:], bv0.partition_broadcast(P)).then_inc(att_in, 16)
            sp.dma_start(x4[:, 1:B, :], xv[:, 1:B, :]).then_inc(x_in, 16)
            sp.dma_start(gate_sb[:], gateT).then_inc(att_in, 16)
            sp.dma_start(gbias_sb[:], gbias.partition_broadcast(P)).then_inc(att_in, 16)

            def step(b):
                for k in range(4):
                    wait(sp, split_l, 4 * b + k - 1)
                    sp.dma_start(stage[:, k % 2, :], wmoe[:, cols(4 * b + k, CHUNK)]).then_inc(chunk_in[k % 2], 16)
                    if k == 1:
                        for dst, src in (late if isinstance(b, int) and b == 0 else []):
                            sp.dma_start(dst, src).then_inc(con_in, 16)
                wait(sp, xq1_ready, b + 1)
                sp.dma_start(xn_d.rearrange("(b p u) n -> b p (u n)", p=P, u=U)[
                    b if isinstance(b, int) else bass.ds(b, 1)], xq1[:] if isinstance(b, int) else
                    xq1[:]).then_inc(xn_stored, 16)

            late = [(wk1_sb[:], wk1), (wv1_sb[:], wv1), (bv1_sb[0:1, :], bv1), (bk1_sb[:], bk1)]
            step(0)
            with sp.Fori(1, B) as b:
                step(b)
            sp.wait_ge(xn_stored, 16 * B)
            xn_b = xn_d.rearrange("(b p u) n -> b p (u n)", p=P, u=U)

            def load_xz(b):
                wait(sp, xz_used, b)
                sp.dma_start(xz[:], xn_b[b if isinstance(b, int) else bass.ds(b, 1)]).then_inc(xz_in, 16)

            def store_y(i):
                for k in range(2):
                    wait(sp, y_kept, 2 * i + k + 1)
                    rows = cols(2 * i + k, P)
                    sp.dma_start(y_d[rows, :], y_sb[:, k, :]).then_inc(y_stored[k], 16)

            store_y(0)
            load_xz(0)
            with sp.Fori(1, B) as i:
                store_y(i)
                load_xz(i)
            with sp.Fori(B, BLOCKS // 2) as i:
                store_y(i)
            sp.wait_ge(y_done, BLOCKS)
            for dst, src in ((wq1_sb, wq1), (bq1_sb, bq1), (wo1_sb, wo1), (wf_sb, wfT)):
                sp.dma_start(dst[:], src).then_inc(l1_in, 16)
            sp.dma_start(bo1_sb[:], bo1.partition_broadcast(P)).then_inc(l1_in, 16)
            sp.dma_start(bf_sb[:], bf.partition_broadcast(P)).then_inc(l1_in, 16)
            out_b = out.rearrange("(b p u) n -> p b (u n)", p=P, u=U)

            def store(i):
                for k in range(2):
                    b = 2 * i + k
                    wait(sp, of_ok, b + 1)
                    sp.dma_start(out_b[:, slice(b, b + 1) if isinstance(b, int) else bass.ds(b, 1), :],
                                 of[:, k:k + 1, :]).then_inc(stored[k], 16)

            with sp.Fori(0, B // 2) as i:
                store(i)
            for k in range(2):
                sp.wait_ge(stored[k], 16 * (B // 2))

        @block.gpsimd
        def _(pool):
            pool.dma_start(ident[:], c_ident).then_inc(cst_in, 16)
            pool.dma_start(gains_sb[:], gains.partition_broadcast(P)).then_inc(cst_in, 16)
            pool.dma_start(tri[:], c_tri).then_inc(cst_in, 16)
            pool.dma_start(count[:], c_count).then_inc(cst_in, 16)
            pool.dma_start(token[:], c_token).then_inc(cst_in, 16)
            pool.dma_start(kmask[:], c_head).then_inc(cst_in, 16)
            pool.memset(half[:], -0.5)
            pool.memset(ones[:], 1.0).then_inc(set_up, 1)
            pool.wait_ge(set_up, 1)

            def root(var_sem, var_t, rstd_t, out_sem, b):
                wait_apart(pool, var_sem, b + 1, pool_tick)
                pool.tensor_tensor(rstd_t[:], var_t[:], half[:], ALU.pow).then_inc(out_sem, 1)

            def step(b, ahead=True):
                if ahead:
                    root(var_ok, var, rstd, rstd_ok, b + 1)
                for k in range(4):
                    if k == 2:
                        root(var1_ok, var1, rstd1, rstd1_ok, b)
                    wait_apart(pool, split_h, 4 * b + k + 1, pool_tick)
                    c = cols(4 * b + k, CHUNK)
                    pool.tensor_tensor(wl[:, c], stage[:, k % 2, :], wh[:, c], ALU.subtract).then_inc(split_l, 1)

            root(var_ok, var, rstd, rstd_ok, 0)
            step(0)
            with pool.Fori(1, B - 1) as b:
                step(b)
            step(B - 1, ahead=False)

            pool.wait_ge(pv_done, B)
            pool.memset(v1[:].rearrange("p (n c) -> p n c", c=HV)[:, :, DK:HV], 1.0).then_inc(ones_ok, 1)
            pool.wait_ge(slots_kept, 1)
            own = Chain(pool, pool_own, pool_tick)

            def gather(i):
                for k in range(2):
                    wait_apart(pool, gathered[k], 16 * i, pool_tick)
                    own.mark(pool.tensor_copy(slot_now[:, k:k + 1], slot_i[:, cols(2 * i + k, 1)]))
                    own.settle_apart()
                    wait_apart(pool, xgT_done, 2 * i + k - 1, pool_tick)
                    pool.indirect_dma_start(xg[:, k, :], None, xn_d, bass.IndirectOffsetOnAxis(
                        ap=slot_now[:, k:k + 1], axis=0)).then_inc(gathered[k], 16)

            gather(0)
            own.loop(1, BLOCKS // 2, 2, gather)
            for k in range(2):
                pool.wait_ge(y_stored[k], 16 * (BLOCKS // 2))
            pool.wait_ge(l1_in, 16 * 6)

            def fetch(b, u):
                for k in range(2):
                    wait_apart(pool, y_here[u], 32 * b, pool_tick)
                    own.mark(pool.tensor_copy(pos_now[:, 2 * u + k:2 * u + k + 1],
                                              pos_i[:, cols((2 * b + u) + k * TILES, 1)]))
                own.settle_apart()
                wait_apart(pool, x2_ok, 2 * b + u - 1, pool_tick)
                for k in range(2):
                    pool.indirect_dma_start(yg[:, 2 * u + k, :], None, y_d, bass.IndirectOffsetOnAxis(
                        ap=pos_now[:, 2 * u + k:2 * u + k + 1], axis=0)).then_inc(y_here[u], 16)

            def root1(var_sem, var_t, rstd_t, out_sem, b, u):
                wait_apart(pool, var_sem, 2 * b + u + 1, pool_tick)
                pool.tensor_tensor(rstd_t[:, 0:1], var_t[:, 0:1], half[:, 0:1], ALU.pow).then_inc(out_sem, 1)

            def keys(b):
                wait_apart(pool, s_done, 8 * b, pool_tick)
                for k in range(2):
                    ins = pool.tensor_tensor(know[:, k], kt1[:, cols(b, C * LK)],
                                             kmask[:, k:k + 1].to_broadcast([P, C * LK]), ALU.mult)
                ins.then_inc(know_ok, 1)

            def slot(b, u, first=False, last=False, end=False):
                if not end:
                    root1(l2_var, var, rstd, l2_rstd, *ahead_of(b, u, 1))
                    if u == 1:
                        keys(b + 1)
                if not last and not end:
                    fetch(*ahead_of(b, u, 2))
                if not first:
                    root1(l3_var, var1, rstd1, l3_rstd, *ahead_of(b, u, -1))
                if not end:
                    nb_, nu = ahead_of(b, u, 1)
                    wait_apart(pool, xn2_ok, 2 * nb_ + nu + 1, pool_tick)
                    t = cols(2 * nb_ + nu, D)
                    pool.tensor_tensor(x_sb[:, t], x_sb[:, t], bo1g[:], ALU.add).then_inc(bo_added, 1)

            pool.wait_ge(bo_ok, 1)
            fetch(0, 0)
            slot(-1, 1, first=True)
            slot(0, 0, first=True)
            slot(0, 1)

            def pair(i):
                slot(i, 0)
                slot(i, 1)

            own.loop(1, B - 1, 4, pair)
            slot(B - 1, 0, last=True)
            slot(B - 1, 1, end=True)
            slot(B, 0, end=True)

        @block.scalar
        def _(act):
            act.wait_ge(cst_in, IN_CST)
            nc.scalar.activation(gain[:], gains_sb[:], ACT.Tanh).then_inc(gain_ok, 1)
            nc.scalar.activation(identb[:], ident[:], ACT.Copy)
            act.wait_ge(att_in, IN_ATT)
            for n, (what, m, h) in enumerate(P0):
                if BY[what] != "act":
                    continue
                act.wait_ge(p0_mm, n + 1)
                if what == "kt0":
                    nc.scalar.activation(kt0[:, m, h * HB:(h + 1) * HB], p0_bank(n)[:, 0:HB], ACT.Identity,
                                         bias=bk0_sb[:, m:m + 1]).then_inc(p0_act, 1)
                else:
                    nc.scalar.activation(bqk[0:1, h * HB:(h + 1) * HB], p0_bank(n)[0:1, 0:HB],
                                         ACT.Copy).then_inc(p0_act, 1)

            def copy_xT(b):
                wait(act, xT_done, b + 1)
                wait_apart(act, scores_done, b, act_tick)
                nc.scalar.activation(xT[:], bank[0][:], ACT.Copy).then_inc(xT_copied, 1)

            def step(b, ahead=True):
                wait(act, max_done, b + 1)
                wait_apart(act, probT_done, b, act_tick)
                for u in range(U):
                    ins = nc.scalar.activation(prob[:, u * LK:(u + 1) * LK], bank[1][:, u * LK:(u + 1) * LK], ACT.Exp,
                                               bias=negmax[:, u:u + 1], accum_out=psum[:, u:u + 1])
                ins.then_inc(exp_done, 1)
                wait(act, probT_done, b + 1)
                wait_apart(act, pv_done, b, act_tick)
                nc.scalar.activation(probT[:], bank[2][0:LK, 0:S], ACT.Copy).then_inc(probT_copied, 1)
                if ahead:
                    copy_xT(b + 1)
                for k in range(4):
                    wait(act, chunk_in[k % 2], 16 * (2 * b + k // 2 + 1))
                    if not isinstance(b, int):
                        act.sem_inc(act_tick, 1)
                    nc.scalar.activation(wh[:, cols(4 * b + k, CHUNK)], stage[:, k % 2, :], ACT.Copy).then_inc(split_h, 1)
                    if k == 1:
                        wait(act, xT1_done, b + 1)
                        wait_apart(act, logit_done, b, act_tick)
                        nc.scalar.activation(xT1[:], bank[4][:], ACT.Copy).then_inc(xT1_copied, 1)

            copy_xT(0)
            step(0)
            with act.Fori(1, B - 1) as b:
                step(b)
            step(B - 1, ahead=False)

            act.wait_ge(con_in, IN_CON)
            act.wait_ge(ones_ok, 1)
            for n, (what, m, h) in enumerate(P1, len(P0)):
                act.wait_ge(p0_mm, n + 1)
                if what == "kt1":
                    nc.scalar.activation(kt1[:].rearrange("p (b c k) -> p b c k", b=B, c=C)[:, h * B // 2:(h + 1) * B // 2, m, :],
                                         p0_bank(n)[:, 0:HB].rearrange("p (b k) -> p b k", k=LK), ACT.Identity,
                                         bias=bk1_sb[:, m:m + 1]).then_inc(p0_act, 1)
                else:
                    nc.scalar.activation(
                        v1[:, m * HEADS * HV:(m + 1) * HEADS * HV].rearrange("p (n c) -> p n c", c=HV)[:, :, 0:DK],
                        p0_bank(n)[0:LK, 0:D].rearrange("p (n c) -> p n c", c=DK), ACT.Copy).then_inc(p0_act, 1)
                if n == len(P0) + 5:
                    act.wait_ge(dif_ok, 1)
                    nc.scalar.activation(ex[:], dif[:], ACT.Exp).then_inc(ex_ok, 1)

            def xh_of(i, k):
                wait(act, xgT_done, 2 * i + k + 1)
                wait(act, h_done, 2 * i + k - 1)
                nc.scalar.activation(xh[:, k, :], bank[k][:, 0:D], ACT.Copy).then_inc(xh_ok, 1)

            def th_of(i, k):
                wait(act, h_done, 2 * i + k + 1)
                wait(act, gate_ok, 2 * i + k)
                nc.scalar.activation(th[:], bank[2 + k][:], ACT.Tanh, scale=0.5).then_inc(th_ok, 1)

            def slot(i, k, last=BLOCKS):
                wait(act, g_done, 2 * i + k + 1)
                wait(act, y_done, 2 * i + k - 1)
                nc.scalar.activation(gh[:, k, :], bank[4 + k][:], ACT.Copy).then_inc(gh_ok, 1)
                if last > 1:
                    th_of(*ahead_of(i, k, 1))
                wait(act, y_done, 2 * i + k + 1)
                wait(act, y_stored[k], 16 * i)
                nc.scalar.activation(y_sb[:, k, :], bank[6 + k][:, 0:D], ACT.Copy).then_inc(y_kept, 1)
                if last > 2:
                    xh_of(*ahead_of(i, k, 2))

            xh_of(0, 0)
            xh_of(0, 1)
            th_of(0, 0)
            slot(0, 0)
            slot(0, 1)
            with act.Fori(1, BLOCKS // 2 - 1) as i:
                slot(i, 0)
                slot(i, 1)
            slot(BLOCKS // 2 - 1, 0, 2)
            slot(BLOCKS // 2 - 1, 1, 1)

            def exp_of(b, u, j):
                wait(act, sub_ok, 8 * b + 4 * u + j + 1)
                nc.scalar.activation(sc[:, j, :], sc[:, j, :], ACT.Exp).then_inc(e_ok, 1)

            def copy_pT(b, u, j):
                wait(act, t_done, 8 * b + 4 * u + j + 1)
                wait(act, pvj_done, 8 * b + 4 * u + j - 3)
                nc.scalar.activation(pT[:, j, :], bank[5 if j else 4][0:LK, :], ACT.Copy).then_inc(pT_ok, 1)

            def copy_oT(b, u):
                wait(act, ot_done, 2 * b + u + 1)
                wait(act, wo_done, 2 * b + u)
                nc.scalar.activation(oT[:], bank[7][:, 0:D], ACT.Copy).then_inc(ot_ok, 1)

            def copy_xT2(b, u):
                wait(act, xt_done, 2 * b + u + 1)
                wait(act, q_done, 2 * b + u)
                nc.scalar.activation(xT2[:], bank[4][:, 0:D], ACT.Copy).then_inc(xt_ok, 1)

            def copy_q(b, u):
                wait(act, q_done, 2 * b + u + 1)
                wait(act, s_done, 8 * b + 4 * u)
                for m in range(C):
                    ins = nc.scalar.activation(qT[:, m * P:(m + 1) * P], bank[4][:, m * P:(m + 1) * P], ACT.Identity,
                                               bias=bq1_sb[:, m:m + 1])
                ins.then_inc(q_ok, 1)

            def slot(b, u, here=True, before=True, after=True):
                if here:
                    exp_of(b, u, 0)
                    exp_of(b, u, 1)
                if before:
                    copy_oT(*ahead_of(b, u, -1))
                if here:
                    copy_pT(b, u, 0)
                    copy_pT(b, u, 1)
                if after:
                    copy_xT2(*ahead_of(b, u, 1))
                if here:
                    exp_of(b, u, 2)
                    copy_pT(b, u, 2)
                if after:
                    copy_q(*ahead_of(b, u, 1))
                if here:
                    exp_of(b, u, 3)
                    copy_pT(b, u, 3)

            act.wait_ge(l1_in, 16 * 6)
            slot(-1, 1, here=False, before=False)
            slot(0, 0, before=False)
            slot(0, 1)
            with act.Fori(1, B - 1) as i:
                slot(i, 0)
                slot(i, 1)
            slot(B - 1, 0)
            slot(B - 1, 1, after=False)
            slot(B, 0, here=False, after=False)

            with act.Fori(0, B) as b:
                wait(act, y8_done, b + 1)
                nc.scalar.activation(y8T[:], bank[2][:].bitcast(BF16)[:, 0:C * S], ACT.Copy).then_inc(y8T_ok, 1)

        @block.vector
        def _(dve):
            own = Chain(dve, dve_own, dve_tick)

            def norm_stats(src, stat_t, mean_t, var_t, out_sem):
                for u in range(U):
                    ins = dve.bn_stats(stat_t[:, u, :], src(u))
                own.mark(ins)
                own.settle_apart()
                for u in range(U):
                    ins = dve.bn_aggr(mean_t[:, u, :], stat_t[:, u, :])
                own.mark(ins)
                own.settle()
                dve.tensor_scalar(var_t[:], mean_t[:, :, 1], EPS, None, ALU.add).then_inc(out_sem, 1)

            def tile_of(b):
                return lambda u: x_sb[:, cols(2 * b + u, D)]

            def ahead_norm(b):
                wait(dve, rstd_ok, b + 1)
                wait_apart(dve, xT_done, b, dve_tick)
                for u in range(U):
                    ins = dve.tensor_scalar(xq[:, u * D:(u + 1) * D], tile_of(b)(u), mean[:, u, 0:1], rstd[:, u:u + 1],
                                            ALU.subtract, ALU.mult)
                ins.then_inc(xq_ready, 1)

            def ahead_max(b):
                wait(dve, scores_done, b + 1)
                wait_apart(dve, exp_done, b, dve_tick)
                dve.tensor_reduce(negmax[:], bank[1][:, 0:U * LK].rearrange("p (u k) -> p u k", u=U), AX, ALU.max,
                                  negate=True).then_inc(max_done, 1)

            def step(b, ahead=True):
                if ahead:
                    norm_stats(tile_of(b + 1), stat, mean, var, var_ok)
                wait(dve, exp_done, b + 1)
                own.mark(dve.reciprocal(rsum[:], psum[:]))
                own.settle()
                own.mark(dve.tensor_scalar(rsumg[:], rsum[:], gain[:, 0:1], None, ALU.mult))
                own.settle()
                if ahead:
                    ahead_norm(b + 1)
                wait(dve, pv_done, b + 1)
                if not isinstance(b, int):
                    dve.sem_inc(dve_tick, 1)
                for u in range(U):
                    ins = dve.scalar_tensor_tensor(tile_of(b)(u), bank[3][:, u * D:(u + 1) * D], rsumg[:, u:u + 1],
                                                   tile_of(b)(u), ALU.mult, ALU.add)
                ins.then_inc(x1_done, 1)
                wait_apart(dve, x1_done, b + 1, dve_tick)
                norm_stats(tile_of(b), stat1, mean1, var1, var1_ok)
                wait(dve, rstd1_ok, b + 1)
                wait(dve, xn_stored, 16 * b)
                wait_apart(dve, xT1_done, b, dve_tick)
                for u in range(U):
                    ins = dve.tensor_scalar(xq1[:, u * D:(u + 1) * D], tile_of(b)(u), mean1[:, u, 0:1],
                                            rstd1[:, u:u + 1], ALU.subtract, ALU.mult)
                ins.then_inc(xq1_ready, 1)
                if ahead:
                    ahead_max(b + 1)
                wait_apart(dve, logit_done, b + 1, dve_tick)
                dve.tensor_tensor(logit[:, cols(b, U * E_ALL)], bank[5][:, 0:U * E_ALL], gbias_sb[:],
                                  ALU.add).then_inc(logit_kept, 1)

            dve.wait_ge(x0_in, 16)
            norm_stats(tile_of(0), stat, mean, var, var_ok)
            ahead_norm(0)
            dve.wait_ge(att_in, IN_ATT)
            for n, (what, m, h) in enumerate(P0):
                if BY[what] != "dve":
                    continue
                dve.wait_ge(p0_mm, n + 1)
                if what == "kq":
                    dve.tensor_copy(kq[:].rearrange("p (b c k) -> p b c k", b=B, c=C)[:, h * B // 2:(h + 1) * B // 2, m, :],
                                    p0_bank(n)[:, 0:HB].rearrange("p (b k) -> p b k", k=LK)).then_inc(p0_dve, 1)
                else:
                    dve.tensor_tensor(v0[:, m * D:(m + 1) * D], p0_bank(n)[0:LK, 0:D], bv0_sb[0:LK, :],
                                      ALU.add).then_inc(p0_dve, 1)
            dve.wait_ge(x_in, 16)
            dve.wait_ge(gain_ok, 1)
            ahead_max(0)
            step(0)
            own.loop(1, B - 1, 6, step)
            step(B - 1, ahead=False)

            def then(ins):
                own.mark(ins)
                own.settle()

            def wide(ap, n):
                return ap.unsqueeze(2).to_broadcast([P, ap.shape[1], n])

            def over(ap, n):
                return ap.unsqueeze(1).to_broadcast([P, n, ap.shape[1]])

            dve.wait_ge(logit_kept, B)
            lg = logit[:].rearrange("p (t e) -> p t e", e=E_ALL)
            numbers = over(count[:, 0:E_ALL], TILES)
            then(dve.tensor_reduce(top[:, 0, :], lg, AX, ALU.max))
            for k in range(2):
                src = lg if k == 0 else left[:]
                then(dve.tensor_tensor(eq[:], src, wide(top[:, k, :], E_ALL), ALU.is_equal))
                then(dve.scalar_tensor_tensor(cand[:], eq[:], -64.0, numbers, ALU.mult, ALU.add))
                then(dve.tensor_reduce(pick[:], cand[:], AX, ALU.min))
                then(dve.tensor_tensor(hot[:, k], cand[:], wide(pick[:], E_ALL), ALU.is_equal))
                if k == 0:
                    then(dve.scalar_tensor_tensor(left[:], hot[:, 0], -3.0e38, lg, ALU.mult, ALU.add))
                    then(dve.tensor_reduce(top[:, 1, :], left[:], AX, ALU.max))
                    dve.tensor_tensor(dif[:], top[:, 1, :], top[:, 0, :], ALU.subtract).then_inc(dif_ok, 1)
            dve.tensor_tensor(pairs[:], hot[:, 0, :, 0:E_FFN], hot[:, 1, :, 0:E_FFN], ALU.add).then_inc(pairs_ok, 1)
            then(dve.tensor_reduce(valid[:].rearrange("p k t -> p (k t)"),
                                   hot[:].rearrange("p k t e -> p (k t) e")[:, :, 0:E_FFN], AX, ALU.add))
            dve.wait_ge(xn_stored, 16 * B)
            dve.wait_ge(split_l, CHUNKS)
            for q in pre:
                ins = dve.memset(q[:, 0:pad, :], 0.0)
            for q in nb:
                ins = dve.memset(q[:, 0:4], 0.0)
            then(ins)
            dve.wait_ge(rank_done, 1)
            then(dve.tensor_copy(pre[0][:, pad:, :], bank[0][:, P:2 * P].rearrange("p (t e) -> p t e", e=E_FFN)))
            a, z = 0, 1
            for n in (1, 2, 4, 8):
                then(dve.tensor_tensor(pre[z][:, pad:, :], pre[a][:, pad:, :], pre[a][:, pad - n:pad + TILES - n, :], ALU.add))
                a, z = z, a
            upto = pre[a]
            then(dve.tensor_scalar(cnt_i[:], upto[:, pad + TILES - 1, :], P - 1.0, None, ALU.add))
            then(dve.tensor_scalar(nb_i[:], cnt_i[:], 7, None, ALU.arith_shift_right))
            then(dve.tensor_copy(nb[0][:, 4:], nb_i[:]))
            then(dve.tensor_scalar(nbk[:], nb[0][:, 4:], float(P), None, ALU.mult))
            a, z = 0, 1
            for n in (1, 2, 4):
                then(dve.tensor_tensor(nb[z][:, 4:], nb[a][:, 4:], nb[a][:, 4 - n:4 + E_FFN - n], ALU.add))
                a, z = z, a
            blocks = nb[a]
            then(dve.scalar_tensor_tensor(nbk[:], blocks[:, 4:], float(P), nbk[:], ALU.mult, ALU.subtract))
            then(dve.tensor_tensor(place[:], bank[0][:, 0:P].rearrange("p (t e) -> p t e", e=E_FFN),
                                   over(nbk[:], TILES), ALU.add))
            then(dve.tensor_tensor(place[:], place[:], upto[:, pad - 1:pad + TILES - 1, :], ALU.add))
            for k in range(2):
                ins = dve.tensor_tensor(prod[:, k], hot[:, k, :, 0:E_FFN], place[:], ALU.mult)
            then(ins)
            then(dve.tensor_reduce(pos[:], prod[:].rearrange("p k t e -> p (k t) e"), AX, ALU.add))
            then(dve.tensor_copy(pos_i[:], pos[:]))
            dve.tensor_scalar(row_i[:], pos_i[:], P - 1, None, ALU.bitwise_and)
            then(dve.tensor_scalar(col_i[:], pos_i[:], 7, None, ALU.arith_shift_right))
            dve.tensor_copy(row[:], row_i[:])
            then(dve.tensor_copy(col[:], col_i[:]))
            then(dve.scalar_tensor_tensor(col[:], col[:], 1.0, valid[:].rearrange("p k t -> p (k t)"), ALU.add, ALU.mult))
            then(dve.tensor_scalar(col[:], col[:], -1.0, None, ALU.add))
            then(dve.tensor_tensor(onecol[:], over(count[:, 0:BLOCKS], 2 * TILES), wide(col[:], BLOCKS), ALU.is_equal))
            dve.tensor_tensor(tokcol[:], onecol[:], wide(token[:], BLOCKS), ALU.mult).then_inc(tok_ok, 1)
            for n in range(4):
                wait(dve, onerow_used, n - 1)
                dve.tensor_tensor(onerow[:, n % 2], over(count[:], 8), wide(row[:, 8 * n:8 * n + 8], P),
                                  ALU.is_equal).then_inc(onerow_ok, 1)
            then(dve.tensor_tensor(cmp[:], over(blocks[:, 4:3 + E_FFN], BLOCKS), wide(count[:, 0:BLOCKS], E_FFN - 1), ALU.is_le))
            then(dve.tensor_reduce(blk[:], cmp[:], AX, ALU.add))
            dve.tensor_copy(blk_i[:], blk[:]).then_inc(blocks_kept, 1)
            dve.wait_ge(slots_done, 1)
            dve.tensor_copy(slot_i[:], bank[1][:, 0:BLOCKS]).then_inc(slots_kept, 1)
            dve.wait_ge(ex_ok, 1)
            then(dve.tensor_scalar(dif[:], ex[:], 1.0, None, ALU.add))
            then(dve.reciprocal(wgt[:, 0, :], dif[:]))
            then(dve.tensor_tensor(wgt[:, 1, :], wgt[:, 0, :], ex[:], ALU.mult))
            then(dve.tensor_tensor(wval[:], wgt[:], valid[:], ALU.mult))
            then(dve.tensor_scalar(cw[:], wval[:].rearrange("p k t -> p (k t)"), gain[:, 1:2], 0.5, ALU.mult, ALU.mult))
            then(dve.tensor_tensor(wgt[:], wgt[:], wval[:], ALU.subtract))
            then(dve.tensor_tensor(cz[:], wgt[:, 0, :], wgt[:, 1, :], ALU.add))
            then(dve.tensor_scalar(cz[:], cz[:], gain[:, 1:2], None, ALU.mult))

            def xl_of(i, k):
                wait(dve, xh_ok, 2 * i + k + 1)
                dve.tensor_tensor(xl[:, k, :], bank[k][:, 0:D], xh[:, k, :], ALU.subtract).then_inc(xl_ok, 1)

            def gate_of(i, k):
                wait(dve, th_ok, 2 * i + k + 1)
                wait(dve, g_done, 2 * i + k - 1)
                dve.scalar_tensor_tensor(gate[:, k, :], th[:], 1.0, bank[2 + k][:], ALU.add, ALU.mult).then_inc(gate_ok, 1)

            def slot(i, k, last=BLOCKS):
                wait(dve, gh_ok, 2 * i + k + 1)
                dve.tensor_tensor(gl[:, k, :], bank[4 + k][:], gh[:, k, :], ALU.subtract).then_inc(gl_ok, 1)
                if last > 1:
                    gate_of(*ahead_of(i, k, 1))
                if last > 2:
                    xl_of(*ahead_of(i, k, 2))

            def pair(i):
                slot(i, 0)
                slot(i, 1)

            def pair_xz(i):
                pair(i)
                wait_apart(dve, xz_in, 16 * i, dve_tick)
                for u in range(U):
                    t = 2 * i + (u - 2)
                    ins = dve.scalar_tensor_tensor(x_sb[:, cols(t, D)], xz[:, u * D:(u + 1) * D], cz[:, cols(t, 1)],
                                                   x_sb[:, cols(t, D)], ALU.mult, ALU.add)
                ins.then_inc(xz_used, 1)

            xl_of(0, 0)
            xl_of(0, 1)
            gate_of(0, 0)
            pair(0)
            with dve.Fori(1, B + 1) as i:
                pair_xz(i)
            with dve.Fori(B + 1, BLOCKS // 2 - 1) as i:
                pair(i)
            slot(BLOCKS // 2 - 1, 0, 2)
            slot(BLOCKS // 2 - 1, 1, 1)

            def combine(b, u):
                t = cols(2 * b + u, D)
                wait(dve, y_here[u], 32 * (b + 1))
                for k in range(2):
                    if k or not isinstance(b, int):
                        dve.sem_inc(dve_tick, 1)
                    ins = dve.scalar_tensor_tensor(x_sb[:, t], yg[:, 2 * u + k, :], cw[:, cols((2 * b + u) + k * TILES, 1)],
                                                   x_sb[:, t], ALU.mult, ALU.add)
                    if k == 0:
                        own.mark(ins)
                        own.settle()
                ins.then_inc(x2_ok, 1)
                wait_apart(dve, x2_ok, 2 * b + u + 1, dve_tick)
                stats1(x_sb[:, t], stat, mean, var, l2_var)

            def stats1(src, stat_t, mean_t, var_t, out_sem):
                own.mark(dve.bn_stats(stat_t[:, 0, :], src))
                own.settle_apart()
                own.mark(dve.bn_aggr(mean_t[:, 0, :], stat_t[:, 0, :]))
                own.settle()
                dve.tensor_scalar(var_t[:, 0:1], mean_t[:, 0, 1:2], EPS, None, ALU.add).then_inc(out_sem, 1)

            def norm2(b, u):
                wait(dve, l2_rstd, 2 * b + u + 1)
                wait_apart(dve, xt_done, 2 * b + u - 1, dve_tick)
                dve.tensor_scalar(xq2[:, u, :], x_sb[:, cols(2 * b + u, D)], mean[:, 0, 0:1], rstd[:, 0:1],
                                  ALU.subtract, ALU.mult).then_inc(xn2_ok, 1)

            def minus_max(b, u, j):
                n = 8 * b + 4 * u + j
                src = bank[j][:, 0:HG * LK].rearrange("p (h k) -> p h k", k=LK)
                wait(dve, s_done, n + 1)
                own.mark(dve.tensor_reduce(nm[:, j * HG:(j + 1) * HG], src, AX, ALU.max, negate=True))
                own.settle()
                wait(dve, t_done, n - 3)
                dve.tensor_tensor(sc[:, j, :].rearrange("p (h k) -> p h k", k=LK), src,
                                  wide(nm[:, j * HG:(j + 1) * HG], LK), ALU.add).then_inc(sub_ok, 1)

            def add_attention(b, u):
                t = cols(2 * b + u, D)
                wait(dve, wo_done, 2 * b + u + 1)
                wait_apart(dve, bo_added, 2 * b + u + 1, dve_tick)
                dve.scalar_tensor_tensor(x_sb[:, t], bank[7][:, 0:D], gain[:, 2:3], x_sb[:, t],
                                         ALU.mult, ALU.add).then_inc(x3_ok, 1)
                wait_apart(dve, x3_ok, 2 * b + u + 1, dve_tick)
                stats1(x_sb[:, t], stat1, mean1, var1, l3_var)

            def divide(b, u):
                o3 = bank[6][:, 0:HEADS * HV].rearrange("p (h c) -> p h c", c=HV)
                wait(dve, pvj_done, 8 * b + 4 * u + 4)
                own.mark(dve.reciprocal(rec[:], o3[:, :, DK]))
                own.settle()
                wait(dve, ot_done, 2 * b + u)
                dve.tensor_tensor(o_sb[:].rearrange("p (h c) -> p h c", c=DK), o3[:, :, 0:DK], wide(rec[:], DK),
                                  ALU.mult).then_inc(on_ok, 1)

            def norm3(b, u):
                t = cols(2 * b + u, D)
                wait_apart(dve, l3_rstd, 2 * b + u + 1, dve_tick)
                own.mark(dve.tensor_scalar(xn_sb[:, t], x_sb[:, t], mean1[:, 0, 0:1], rstd1[:, 0:1],
                                           ALU.subtract, ALU.mult))
                own.settle_apart()
                dve.tensor_reduce(amx[:, cols(2 * b + u, 1)], xn_sb[:, t], AX, ALU.max,
                                  apply_absolute_value=True).then_inc(amax_ok, 1)

            def slot(b, u, here=True, before=True, after=True):
                if after:
                    combine(*ahead_of(b, u, 1))
                if here:
                    minus_max(b, u, 0)
                    minus_max(b, u, 1)
                if after:
                    norm2(*ahead_of(b, u, 1))
                if here:
                    minus_max(b, u, 2)
                    minus_max(b, u, 3)
                if before:
                    add_attention(*ahead_of(b, u, -1))
                if here:
                    divide(b, u)
                if before:
                    norm3(*ahead_of(b, u, -1))

            def pair(i):
                slot(i, 0)
                slot(i, 1)

            dve.wait_ge(l1_in, 16 * 6)
            dve.tensor_scalar(bo1g[:], bo1_sb[:], gain[:, 2:3], None, ALU.mult).then_inc(bo_ok, 1)
            slot(-1, 1, here=False, before=False)
            slot(0, 0, before=False)
            slot(0, 1)
            own.loop(1, B - 1, 2 * 11, pair)
            slot(B - 1, 0)
            slot(B - 1, 1, after=False)
            slot(B, 0, here=False, after=False)

            dve.wait_ge(amax_ok, TILES)
            dve.tensor_reduce(red[:, 0:1], amx[:], AX, ALU.max)
            dve.tensor_reduce(red[:, 1:2], wf_sb[:], AX, ALU.max, apply_absolute_value=True).then_inc(red_ok, 1)
            dve.wait_ge(red_done, 1)
            then(dve.tensor_reduce(peak[:], bank[0][0:2, 0:P], AX, ALU.max))
            dve.tensor_scalar(peaks[:], ident[0:2, 0:2], peak[:, 0:1], None, ALU.mult).then_inc(peak_ok, 1)
            dve.wait_ge(peak_done, 1)
            then(dve.tensor_scalar(red[:, 2:4], bank[1][:, 0:2], 1e-12, None, ALU.max))
            then(dve.reciprocal(red[:, 4:6], red[:, 2:4]))
            then(dve.tensor_scalar(red[:, 6:8], red[:, 4:6], FP8_MAX, FP8_MAX, ALU.mult, ALU.min))
            then(dve.reciprocal(red[:, 8:10], red[:, 6:8]))
            then(dve.tensor_scalar(red[:, 10:11], red[:, 8:9], red[:, 9:10], None, ALU.mult))

            def to_f8(dst, src, scale, apart):
                if apart:
                    dve.sem_inc(dve_tick, 1)
                then(dve.tensor_scalar(yq[:], src, scale, FP8_MAX, ALU.mult, ALU.min))
                then(dve.tensor_scalar(ye[:], yq[:].bitcast(I32), 0x7F800000, None, ALU.bitwise_and))
                then(dve.tensor_scalar(ym[:], ye[:].bitcast(F32), TINY, MAGIC, ALU.max, ALU.mult))
                then(dve.scalar_tensor_tensor(yt[:], yq[:], -FP8_MAX, ym[:], ALU.max, ALU.add))
                return dve.tensor_tensor(dst, yt[:], ym[:], ALU.subtract)

            def quantise(b):
                wait(dve, y8_done, b)
                to_f8(y8[:], xn_sb[:, cols(b, U * D)], red[:, 6:7], not isinstance(b, int)).then_inc(y8_ok, 1)

            def finish(b, k):
                wait(dve, acc_done, b + 1)
                then(dve.scalar_tensor_tensor(zf[:, k, :].rearrange("p (u n) -> p u n", u=U),
                                              bank[4 + k][:].rearrange("p (u n) -> p u n", u=U), red[:, 10:11],
                                              over(bf_sb[:], U), ALU.mult, ALU.add))
                wait(dve, stored[k], 16 * ((b - k) // 2) if isinstance(b, int) else None) if isinstance(b, int) else None
                if not isinstance(b, int):
                    wait_apart(dve, stored[k], (b - k) * 8, dve_tick)
                dve.scalar_tensor_tensor(of[:, k, :], zf[:, k, :], gain[:, 3:4], x_sb[:, cols(b, U * D)],
                                         ALU.mult, ALU.add).then_inc(of_ok, 1)

            to_f8(wf8[:], wf_sb[:], red[:, 7:8], False).then_inc(wf8_ok, 1)
            dve.wait_ge(wf8_ok, 1)
            quantise(0)

            def pair(i):
                for k in range(2):
                    quantise(2 * i + (k + 1))
                    finish(2 * i + k, k)

            pair(0)
            own.loop(1, B // 2 - 1, 10, pair)
            b = B - 2
            quantise(b + 1)
            finish(b, 0)
            finish(b + 1, 1)

        @block.tensor
        def _(pe):
            def free_bank(n):
                if n >= 4:
                    who, k = evacuated(n - 4)
                    pe.wait_ge(p0_act if who == "act" else p0_dve, k)

            pe.wait_ge(att_in, IN_ATT)
            pe.wait_ge(cst_in, IN_CST)

            def transposes(dst, src):
                for c in range(C):
                    for u in range(U):
                        ins = pe.transpose(dst[:, c * S + u * P:c * S + u * P + P],
                                           src[:, u * D + c * P:u * D + c * P + P], ident[:])
                return ins

            def ahead_xT(b):
                wait(pe, xq_ready, b + 1)
                wait(pe, xT_copied, b)
                transposes(bank[0], xq).then_inc(xT_done, 1)

            def ahead_scores(b):
                wait(pe, xT_copied, b + 1)
                wait(pe, exp_done, b)
                for u in range(U):
                    dst = bank[1][:, u * LK:(u + 1) * LK]
                    for c in range(C):
                        k = slice(b * C * LK + c * LK, b * C * LK + c * LK + LK) if isinstance(b, int) \
                            else bass.ds(b * (C * LK) + c * LK, LK)
                        pe.matmul(dst, xT[:, c * S + u * P:c * S + u * P + P], kq[:, k], start=(c == 0), stop=False)
                    ins = pe.matmul(dst, ones[0:1, :], bqk[0:1, cols(b, LK)], start=False, stop=True)
                ins.then_inc(scores_done, 1)

            for n, (what, m, h) in enumerate(P0):
                free_bank(n)
                hs = slice(h * HB, (h + 1) * HB)
                if what == "kt0":
                    ins = pe.matmul(p0_bank(n)[:, 0:HB], wk0_sb[:, m * P:(m + 1) * P], ctxT_sb[:, hs], start=True, stop=True)
                if what == "kq":
                    if n == 4:
                        pe.wait_ge(p0_act, 4)
                    for c in range(C):
                        ins = pe.matmul(p0_bank(n)[:, 0:HB], wq0_sb[:, c, m * P:(m + 1) * P], kt0[:, c, hs],
                                        start=(c == 0), stop=(c == C - 1))
                if what == "bqk":
                    for c in range(C):
                        ins = pe.matmul(p0_bank(n)[0:1, 0:HB], bq0_sb[:, c:c + 1], kt0[:, c, hs],
                                        start=(c == 0), stop=(c == C - 1))
                if what == "v0":
                    ins = pe.matmul(p0_bank(n)[0:LK, 0:D], ctxT_sb[:, m * LK:(m + 1) * LK], wv0_sb[:], start=True, stop=True)
                ins.then_inc(p0_mm, 1)
            pe.wait_ge(p0_act, 6)
            pe.wait_ge(p0_dve, 12)
            pe.wait_ge(set_up, 1)

            def step(b, ahead=True):
                wait(pe, exp_done, b + 1)
                wait(pe, probT_copied, b)
                for u in range(U):
                    ins = pe.transpose(bank[2][0:LK, u * P:(u + 1) * P], prob[:, u * LK:(u + 1) * LK], ident[:])
                ins.then_inc(probT_done, 1)
                if ahead:
                    ahead_xT(b + 1)
                wait(pe, probT_copied, b + 1)
                wait(pe, x1_done, b)
                for u in range(U):
                    ins = pe.matmul(bank[3][:, u * D:(u + 1) * D], probT[:, u * P:(u + 1) * P], v0[:, cols(b, D)],
                                    start=True, stop=True)
                ins.then_inc(pv_done, 1)
                if ahead:
                    ahead_scores(b + 1)
                wait(pe, xq1_ready, b + 1)
                wait(pe, xT1_copied, b)
                transposes(bank[4], xq1).then_inc(xT1_done, 1)
                wait(pe, xT1_copied, b + 1)
                wait(pe, logit_kept, b)
                for u in range(U):
                    for c in range(C):
                        ins = pe.matmul(bank[5][:, u * E_ALL:(u + 1) * E_ALL], xT1[:, c * S + u * P:c * S + u * P + P],
                                        gate_sb[:, c, :], start=(c == 0), stop=(c == C - 1))
                ins.then_inc(logit_done, 1)

            ahead_xT(0)
            ahead_scores(0)
            step(0)
            with pe.Fori(1, B - 1) as b:
                step(b)
            step(B - 1, ahead=False)

            pe.wait_ge(con_in, IN_CON)
            pe.wait_ge(logit_kept, B)
            for n, (what, m, h) in enumerate(P1, len(P0)):
                if n >= len(P0) + 4:
                    free_bank(n)
                if what == "kt1":
                    ins = pe.matmul(p0_bank(n)[:, 0:HB], wk1_sb[:, m * P:(m + 1) * P], ctxT_sb[:, h * HB:(h + 1) * HB],
                                    start=True, stop=True)
                else:
                    pe.matmul(p0_bank(n)[0:LK, 0:D], ctxT_sb[:, m * LK:(m + 1) * LK], wv1_sb[:], start=True, stop=False)
                    ins = pe.matmul(p0_bank(n)[0:LK, 0:D], ones[0:1, 0:LK], bv1_sb[0:1, :], start=False, stop=True)
                ins.then_inc(p0_mm, 1)
                if n == len(P0) + 5:
                    pe.wait_ge(pairs_ok, 1)
                    pm = pairs[:].rearrange("p t e -> p (t e)")
                    pe.matmul(bank[0][:, 0:P], tri[:, 0:P], pm, start=True, stop=True)
                    pe.matmul(bank[0][:, P:2 * P], tri[:, P:2 * P], pm, start=True, stop=True).then_inc(rank_done, 1)
            pe.wait_ge(tok_ok, 1)
            for n in range(4):
                pe.wait_ge(onerow_ok, n + 1)
                for m in range(8):
                    ins = pe.matmul(bank[1][:, 0:BLOCKS], onerow[:, n % 2, m, :], tokcol[:, 8 * n + m, :],
                                    start=(n == m == 0), stop=(n == 3 and m == 7))
                ins.then_inc(onerow_used if n < 3 else slots_done, 1)
            pe.wait_ge(split_l, CHUNKS)
            pe.wait_ge(blocks_kept, 1)
            pe.wait_ge(slots_kept, 1)
            pe.wait_ge(p0_act, 18)

            def expert(i, k):
                return pe.value_load(blk_i[0:1, cols(2 * i + k, 1)], min_val=0, max_val=E_FFN - 1) * WE

            def xT_of(i, k):
                wait(pe, gathered[k], 16 * (i + 1))
                wait(pe, xl_ok, 2 * i + k - 1)
                for c in range(C):
                    ins = pe.transpose(bank[k][:, c * P:(c + 1) * P], xg[:, k, c * P:(c + 1) * P], ident[:])
                ins.then_inc(xgT_done, 1)

            def three(dst, ah, al, w, n, first, last):
                pe.matmul(dst, ah, wh[:, bass.ds(w, n)], start=first, stop=False)
                pe.matmul(dst, ah, wl[:, bass.ds(w, n)], start=False, stop=False)
                return pe.matmul(dst, al, wh[:, bass.ds(w, n)], start=False, stop=last)

            def h_of(i, k):
                e = expert(i, k)
                wait(pe, xl_ok, 2 * i + k + 1)
                wait(pe, gate_ok, 2 * i + k - 1)
                for c in range(C):
                    ins = three(bank[2 + k][:], xh[:, k, c * P:(c + 1) * P], xl[:, k, c * P:(c + 1) * P], e + c * FF, FF,
                                c == 0, c == C - 1)
                ins.then_inc(h_done, 1)

            def slot(i, k, last=BLOCKS):
                wait(pe, gate_ok, 2 * i + k + 1)
                wait(pe, gl_ok, 2 * i + k - 1)
                for c in range(FC):
                    ins = pe.transpose(bank[4 + k][:, c * P:(c + 1) * P], gate[:, k, c * P:(c + 1) * P], ident[:])
                ins.then_inc(g_done, 1)
                if last > 1:
                    h_of(*ahead_of(i, k, 1))
                e = expert(i, k)
                wait(pe, gl_ok, 2 * i + k + 1)
                wait(pe, y_kept, 2 * i + k - 1)
                for c in range(FC):
                    ins = three(bank[6 + k][:, 0:D], gh[:, k, c * P:(c + 1) * P], gl[:, k, c * P:(c + 1) * P],
                                e + (C * FF + c * D), D, c == 0, c == FC - 1)
                ins.then_inc(y_done, 1)
                if last > 2:
                    xT_of(*ahead_of(i, k, 2))

            xT_of(0, 0)
            xT_of(0, 1)
            h_of(0, 0)
            slot(0, 0)
            slot(0, 1)
            with pe.Fori(1, BLOCKS // 2 - 1) as i:
                slot(i, 0)
                slot(i, 1)
            slot(BLOCKS // 2 - 1, 0, 2)
            slot(BLOCKS // 2 - 1, 1, 1)

            def heads_of(j):
                return [(c, k, 2 * NB * c + 2 * j + k) for c in range(C) for k in range(2)]

            def transpose_p(b, u, j):
                wait(pe, e_ok, 8 * b + 4 * u + j + 1)
                if j == 0:
                    wait(pe, q_ok, 2 * b + u + 1)
                else:
                    wait(pe, pT_ok, 8 * b + 4 * u + (j if j > 1 else 0))
                for n in range(HG):
                    ins = pe.transpose(bank[5 if j else 4][0:LK, n * P:(n + 1) * P], sc[:, j, n * LK:(n + 1) * LK], ident[:])
                ins.then_inc(t_done, 1)

            def values(b, u, j):
                wait(pe, pT_ok, 8 * b + 4 * u + j + 1)
                if j == 0:
                    wait(pe, on_ok, 2 * b + u)
                for n, (_, _, h) in enumerate(heads_of(j)):
                    at = slice(b * HEADS * HV + h * HV, b * HEADS * HV + h * HV + HV) if isinstance(b, int) \
                        else bass.ds(b * (HEADS * HV) + h * HV, HV)
                    ins = pe.matmul(bank[6][:, h * HV:(h + 1) * HV], pT[:, j, n * P:(n + 1) * P], v1[:, at],
                                    start=True, stop=True)
                ins.then_inc(pvj_done, 1)

            def transpose_x(b, u):
                wait(pe, xn2_ok, 2 * b + u + 1)
                wait(pe, pT_ok, 8 * b + 4 * u - 3)
                for c in range(C):
                    ins = pe.transpose(bank[4][:, c * P:(c + 1) * P], xq2[:, u, c * P:(c + 1) * P], ident[:])
                ins.then_inc(xt_done, 1)

            def queries(b, u):
                wait(pe, xt_ok, 2 * b + u + 1)
                for m in range(C):
                    for c in range(C):
                        ins = pe.matmul(bank[4][:, m * P:(m + 1) * P], wq1_sb[:, c, m * P:(m + 1) * P],
                                        xT2[:, c * P:(c + 1) * P], start=(c == 0), stop=(c == C - 1))
                ins.then_inc(q_done, 1)

            def scores(b, u):
                wait(pe, q_ok, 2 * b + u + 1)
                wait(pe, know_ok, b + 1)
                for j in range(NB):
                    wait(pe, sub_ok, 8 * b + 4 * u + j - 3)
                    g = slice(32 * j, 32 * j + 32)
                    for n, (c, k, _) in enumerate(heads_of(j)):
                        ins = pe.matmul(bank[j][:, n * LK:(n + 1) * LK], qT[g, c * P:(c + 1) * P],
                                        know[g, k, c * LK:(c + 1) * LK], start=True, stop=True)
                    ins.then_inc(s_done, 1)

            def transpose_o(b, u):
                wait(pe, on_ok, 2 * b + u + 1)
                wait(pe, x3_ok, 2 * b + u)
                for c in range(C):
                    ins = pe.transpose(bank[7][:, c * P:(c + 1) * P], o_sb[:, c * P:(c + 1) * P], ident[:])
                ins.then_inc(ot_done, 1)

            def project(b, u):
                wait(pe, ot_ok, 2 * b + u + 1)
                for c in range(C):
                    ins = pe.matmul(bank[7][:, 0:D], oT[:, c * P:(c + 1) * P], wo1_sb[:, c, :],
                                    start=(c == 0), stop=(c == C - 1))
                ins.then_inc(wo_done, 1)

            def slot(b, u, here=True, before=True, after=True):
                if before:
                    transpose_o(*ahead_of(b, u, -1))
                if here:
                    transpose_p(b, u, 0)
                    transpose_p(b, u, 1)
                if before:
                    project(*ahead_of(b, u, -1))
                if here:
                    values(b, u, 0)
                if after:
                    transpose_x(*ahead_of(b, u, 1))
                if here:
                    transpose_p(b, u, 2)
                    values(b, u, 1)
                if after:
                    queries(*ahead_of(b, u, 1))
                if here:
                    transpose_p(b, u, 3)
                    values(b, u, 2)
                    values(b, u, 3)
                if after:
                    scores(*ahead_of(b, u, 1))

            pe.wait_ge(l1_in, 16 * 6)
            pe.wait_ge(y_kept, BLOCKS)
            slot(-1, 1, here=False, before=False)
            slot(0, 0, before=False)
            slot(0, 1)
            with pe.Fori(1, B - 1) as i:
                slot(i, 0)
                slot(i, 1)
            slot(B - 1, 0)
            slot(B - 1, 1, after=False)
            slot(B, 0, here=False, after=False)

            pe.wait_ge(red_ok, 1)
            pe.transpose(bank[0][0:2, 0:P], red[:, 0:2], ident[:]).then_inc(red_done, 1)
            pe.wait_ge(peak_ok, 1)
            pe.matmul(bank[1][:, 0:2], ones[:], peaks[:], start=True, stop=True).then_inc(peak_done, 1)
            pe.wait_ge(wf8_ok, 1)
            with pe.Fori(0, B // 2) as i:
                for k in range(2):
                    b = 2 * i + k
                    wait(pe, y8_ok, b + 1)
                    dst = bank[2][:].bitcast(BF16)
                    for c in range(C):
                        for u in range(U):
                            ins = pe.transpose(dst[:, c * S + u * P:c * S + u * P + P],
                                               y8[:, u * D + c * P:u * D + c * P + P], identb[:])
                    ins.then_inc(y8_done, 1)
                    wait(pe, y8T_ok, b + 1)
                    wait(pe, of_ok, b - 1) if isinstance(b, int) else None
                    for u in range(U):
                        for c in range(C):
                            ins = pe.matmul(bank[4 + k][:, u * D:(u + 1) * D], y8T[:, c * S + u * P:c * S + u * P + P],
                                            wf8[:, c * D:(c + 1) * D], start=(c == 0), stop=(c == C - 1))
                    ins.then_inc(acc_done, 1)


def kernel(**inputs):
    import concourse.bacc as bacc
    import ml_dtypes
    from concourse.bass_utils import run_bass_kernel_spmd

    a = {k: np.asarray(v) for k, v in inputs.items()}

    def chunked(w):
        return w.reshape(-1, P, w.shape[-1]).transpose(1, 0, 2)

    w1 = a["L0_ffn_w1"].transpose(0, 2, 1).reshape(E_FFN, C, P, FF).transpose(2, 0, 1, 3).reshape(P, E_FFN, C * FF)
    w2 = a["L0_ffn_w2"].transpose(0, 2, 1).reshape(E_FFN, FC, P, D).transpose(2, 0, 1, 3).reshape(P, E_FFN, FC * D)
    p, t = np.arange(P)[:, None], np.arange(2 * TILES)[None, :] % TILES
    tri = np.concatenate([np.triu(np.ones((P, P)), 1), np.ones((P, P))], axis=1)
    arrays = dict(
        x=a["x"].reshape(B * S, D), ctxT=a["ctx_512"].transpose(2, 0, 1).reshape(-1, B * LK),
        wq0T=chunked(a["L0_xattn_Wq"].T), wk0=a["L0_xattn_Wk"], wv0=a["L0_xattn_Wv"],
        bq0=a["L0_xattn_bq"].reshape(C, P).T, bk0=a["L0_xattn_bk"].reshape(C, P).T, bv0=a["L0_xattn_bv"],
        gateT=chunked(a["L0_ffn_gate_w"].T), gbias=np.tile(a["L0_ffn_expert_bias"], U),
        wmoe=np.concatenate([w1, w2], axis=2).reshape(P, -1),
        wq1=chunked(a["L1_xattn_Wq"]), wk1=a["L1_xattn_Wk"], wv1=a["L1_xattn_Wv"], wo1=chunked(a["L1_xattn_Wo"]),
        bq1=a["L1_xattn_bq"].reshape(C, P).T, bk1=a["L1_xattn_bk"].reshape(C, P).T, bv1=a["L1_xattn_bv"].reshape(1, D),
        bo1=a["L1_xattn_bo"], wfT=chunked(a["L1_ffn_weight"].T).reshape(P, C * D), bf=a["L1_ffn_bias"],
        gains=np.stack([a["g_xattn"], a["g_ffn"]], axis=1).reshape(-1),
        c_ident=np.eye(P, dtype=np.float32), c_tri=tri.astype(ml_dtypes.bfloat16),
        c_count=np.tile(np.arange(P, dtype=np.float32), (P, 1)),
        c_token=(t // U * S + U * p + t % U).astype(np.float32),
        c_head=np.stack([(p[:, 0] // DK % 2 == 0) * 0.25, (p[:, 0] // DK % 2 == 1) * 0.25], axis=1).astype(np.float32),
    )
    nc = bacc.Bacc("TRN2", target_bir_lowering=False, num_devices=1)
    args = {}
    for name in arrays:
        arrays[name] = np.ascontiguousarray(arrays[name])
        args[name] = nc.dram_tensor(f"in_{name}", arrays[name].shape, mybir.dt.from_np(arrays[name].dtype),
                                    kind="ExternalInput").ap()
    out = nc.dram_tensor("out_x", (B * S, D), F32, kind="ExternalOutput").ap()
    build(nc, out=out, **args)
    r = run_bass_kernel_spmd(nc, [{f"in_{k}": v for k, v in arrays.items()}], core_ids=[0])
    return r.results[0]["out_x"].reshape(B, S, D)
```

```python
from contextlib import ExitStack

import concourse.bass as bass
import numpy as np
from concourse import mybir

ALU = mybir.AluOpType
ACT = mybir.ActivationFunctionType
AX = mybir.AxisListType.X
F32, F32R, BF16, F16, I32 = (mybir.dt.float32, mybir.dt.float32r, mybir.dt.bfloat16, mybir.dt.float16,
                             mybir.dt.int32)

P = 128
B, S, D = 8, 256, 256
LK = 120
U = S // P
TILES = B * U
C = D // P
E_ALL, E_FFN, FF = 12, 8, 512
FC = FF // P
WE = C * FF + FC * D
CHUNK = 512
CHUNKS = E_FFN * WE // CHUNK
STAGES = 4
GROUPS = CHUNKS // STAGES
LEAD = 2
BLOCKS = 2 * TILES + E_FFN
HEADS, DK = 16, 16
NB = 4
HG = HEADS // NB
EPS = 1e-5
FP8_MAX = 448.0
MAGIC = 1.5 * 2.0 ** 20
TINY = 2.0 ** -6


class Chain:

    def __init__(self, eng, sem, tick):
        self.eng, self.sem, self.tick, self.n, self.seen = eng, sem, tick, 0, 0

    def mark(self, ins):
        ins.then_inc(self.sem, 1)
        self.n = self.n + 1
        self.seen += 1

    def settle(self):
        self.eng.wait_ge(self.sem, self.n)

    def settle_apart(self):
        wait_apart(self.eng, self.sem, self.n, self.tick)

    def loop(self, first, last, per, body):
        base = self.n
        with self.eng.Fori(first, last) as i:
            self.n, self.seen = i * per + (base - first * per), 0
            body(i)
            assert self.seen == per, (self.seen, per)
        self.n = base + per * (last - first)


def wait(eng, sem, value):
    if not isinstance(value, int) or value > 0:
        eng.wait_ge(sem, value)


def wait_apart(eng, sem, value, tick):
    wait(eng, sem, value)
    if not isinstance(value, int):
        eng.sem_inc(tick, 1)


def cols(i, n):
    return slice(i * n, i * n + n) if isinstance(i, int) else bass.ds(i * n, n)


def build(nc, x, ctxT, wq0T, wk0, wv0, bq0, bk0, bv0, gateT, gbias, wmoe, wq1, wk1, wv1, wo1,
          bq1, bk1, bv1, bo1, wfT, bf, gains, c_ident, c_tri, c_count, c_token, c_head, out):
    ctx = ExitStack()
    with ctx:
        HB = B // 2 * LK

        def sb(name, shape, dt=F32, stack=ctx):
            return stack.enter_context(nc.sbuf_tensor(name, shape, dt))

        def sem(name):
            return ctx.enter_context(nc.semaphore(name))

        bank = [ctx.enter_context(nc.psum_tensor(f"bank{i}", [P, 512], F32)) for i in range(8)]
        xn_d = nc.dram_tensor("xn_d", [B * S, D], F32).ap()
        y_d = nc.dram_tensor("y_d", [BLOCKS * P, D], F32).ap()

        x_sb = sb("x_sb", [P, TILES * D])
        ident = sb("ident", [P, P])
        identb = sb("identb", [P, P], BF16)
        gains_sb = sb("gains_sb", [P, 4])
        gain = sb("gain", [P, 4])
        ones = sb("ones", [2, P])
        half = sb("half", [P, U])
        cw = sb("cw", [P, 2 * TILES])
        cz = sb("cz", [P, TILES])
        pos_i = sb("pos_i", [P, 2 * TILES], I32)
        slot_i = sb("slot_i", [P, BLOCKS], I32)
        blk_i = sb("blk_i", [P, BLOCKS // 2], I32)
        pos_now = sb("pos_now", [P, 4], I32)
        slot_now = sb("slot_now", [P, 2], I32)
        stat = sb("stat", [P, U, 6])
        mean = sb("mean", [P, U, 2])
        var = sb("var", [P, U])
        rstd = sb("rstd", [P, U])
        stat1 = sb("stat1", [P, U, 6])
        mean1 = sb("mean1", [P, U, 2])
        var1 = sb("var1", [P, U])
        rstd1 = sb("rstd1", [P, U])
        bk1_sb = sb("bk1_sb", [P, C])
        kmask = sb("kmask", [P, 2])
        wo1_sb = sb("wo1_sb", [P, C, D])
        bq1_sb = sb("bq1_sb", [P, C])
        bf_sb = sb("bf_sb", [P, D])
        wf_sb = sb("wf_sb", [P, C * D])
        red = sb("red", [P, 16])
        peak = sb("peak", [1, 2])
        kv = ExitStack()
        kq = sb("kq", [P, B * C * LK], F32, kv)
        v0 = sb("v0", [LK, B * D], F32, kv)
        bqk = sb("bqk", [1, B * LK], F32, kv)
        kv.close()
        kt1 = sb("kt1", [P, C * B * LK])
        v1 = sb("v1", [LK, B * D])
        wq1_sb = sb("wq1_sb", [P, C, D])
        bo1_sb = sb("bo1_sb", [P, D])
        fill = sb("fill", [P, B * LK - (C + 1) * D])
        moe = ExitStack()
        wh = sb("wh", [P, E_FFN * WE], F32R, moe)
        wl = sb("wl", [P, E_FFN * WE], F32R, moe)
        con = ExitStack()
        ctxT_sb = sb("ctxT_sb", [P, B * LK], F32, con)
        wk1_sb = sb("wk1_sb", [P, D], F32, con)
        wv1_sb = sb("wv1_sb", [P, D], F32, con)
        bv1_sb = sb("bv1_sb", [P, D], F32, con)
        tri = sb("tri", [P, 2 * P], BF16, con)
        count = sb("count", [P, P], F32, con)
        token = sb("token", [P, 2 * TILES], F32, con)
        logit = sb("logit", [P, TILES * E_ALL], F32, con)
        att = ExitStack()
        wq0_sb = sb("wq0_sb", [P, C, D], F32, att)
        wk0_sb = sb("wk0_sb", [P, D], F32, att)
        wv0_sb = sb("wv0_sb", [P, D], F32, att)
        bq0_sb = sb("bq0_sb", [P, C], F32, att)
        bk0_sb = sb("bk0_sb", [P, C], F32, att)
        bv0_sb = sb("bv0_sb", [P, D], F32, att)
        gate_sb = sb("gate_sb", [P, C, P], F32, att)
        gbias_sb = sb("gbias_sb", [P, U * E_ALL], F32, att)
        negmax = sb("negmax", [P, U], F32, att)
        psum = sb("psum", [P, U], F32, att)
        rsum = sb("rsum", [P, U], F32, att)
        rsumg = sb("rsumg", [P, U], F32, att)
        stage = sb("stage", [P, STAGES, CHUNK], F32, att)
        xq = sb("xq", [P, U * D], F32, att)
        kt0 = sb("kt0", [P, C, HB], F32, att)
        xT = sb("xT", [P, C * S], F32, att)
        prob = sb("prob", [P, U * LK], F32, att)
        probT = sb("probT", [LK, S], F32, att)
        xq1 = sb("xq1", [P, U * D], F32, att)
        xT1 = sb("xT1", [P, C * S], F32, att)
        att.close()
        rt = ExitStack()
        V3 = [P, TILES, E_ALL]
        eq = sb("eq", V3, F32, rt)
        cand = sb("cand", V3, F32, rt)
        left = sb("left", V3, F32, rt)
        hot = sb("hot", [P, 2, TILES, E_ALL], F32, rt)
        top = sb("top", [P, 2, TILES], F32, rt)
        pick = sb("pick", [P, TILES], F32, rt)
        dif = sb("dif", [P, TILES], F32, rt)
        ex = sb("ex", [P, TILES], F32, rt)
        wgt = sb("wgt", [P, 2, TILES], F32, rt)
        valid = sb("valid", [P, 2, TILES], F32, rt)
        wval = sb("wval", [P, 2, TILES], F32, rt)
        pairs = sb("pairs", [P, TILES, E_FFN], BF16, rt)
        pad = TILES // 2
        pre = [sb(f"pre{i}", [P, pad + TILES, E_FFN], F32, rt) for i in range(2)]
        cnt_i = sb("cnt_i", [P, E_FFN], I32, rt)
        nb_i = sb("nb_i", [P, E_FFN], I32, rt)
        nb = [sb(f"nb{i}", [P, 4 + E_FFN], F32, rt) for i in range(2)]
        nbk = sb("nbk", [P, E_FFN], F32, rt)
        place = sb("place", [P, TILES, E_FFN], F32, rt)
        prod = sb("prod", [P, 2, TILES, E_FFN], F32, rt)
        pos = sb("pos", [P, 2 * TILES], F32, rt)
        row_i = sb("row_i", [P, 2 * TILES], I32, rt)
        col_i = sb("col_i", [P, 2 * TILES], I32, rt)
        row = sb("row", [P, 2 * TILES], F32, rt)
        col = sb("col", [P, 2 * TILES], F32, rt)
        onerow = sb("onerow", [P, 2, 8, P], F16, rt)
        onecol = sb("onecol", [P, 2 * TILES, BLOCKS], F16, rt)
        tokcol = sb("tokcol", [P, 2 * TILES, BLOCKS], F16, rt)
        cmp = sb("cmp", [P, BLOCKS + 2, E_FFN - 1], F32, rt)
        blk = sb("blk", [P, BLOCKS + 2], F32, rt)
        blks = sb("blks", [P, 2, BLOCKS // 2], F32, rt)
        rt.close()
        con.close()
        ex_ = ExitStack()
        xg = sb("xg", [P, 2, D], F32, ex_)
        xh = sb("xh", [P, 2, D], F32R, ex_)
        xl = sb("xl", [P, 2, D], F32R, ex_)
        th = sb("th", [P, FF], F32, ex_)
        gate = sb("gate", [P, 2, FF], F32, ex_)
        gh = sb("gh", [P, 2, FF], F32R, ex_)
        gl = sb("gl", [P, 2, FF], F32R, ex_)
        y_sb = sb("y_sb", [P, 2, D], F32, ex_)
        xz = sb("xz", [P, U * D], F32, ex_)
        ex_.close()
        moe.close()
        xn_sb = sb("xn_sb", [P, TILES * D])
        bo1g = sb("bo1g", [P, D])
        wf8 = sb("wf8", [P, C * D], BF16)
        kpart = sb("kpart", [P, 2, C * LK])
        know = sb("know", [P, 2 * C, 2, LK], F32R)
        yg = sb("yg", [P, 4, D])
        xq2 = sb("xq2", [P, 2, D])
        xT2 = sb("xT2", [P, D])
        qh = sb("qh", [P, U, D], F32R)
        ql = sb("ql", [P, U, D], F32R)
        nm = sb("nm", [P, HEADS])
        sc = sb("sc", [P, NB, HG * LK])
        pT = sb("pT", [LK, NB, HG * P])
        ssum = sb("ssum", [P, U, HEADS])
        rec1 = sb("rec1", [P, HEADS])
        rec = sb("rec", [P, HEADS, DK])
        recT = sb("recT", [P, D])
        vnow = sb("vnow", [LK, HEADS, P])
        oT = sb("oT", [P, D])
        amx = sb("amx", [P, TILES])
        yq = sb("yq", [P, 2 * D])
        ye = sb("ye", [P, 2 * D], I32)
        ym = sb("ym", [P, 2, 2 * D])
        yt = sb("yt", [P, 2, 2 * D])
        y8 = sb("y8", [P, 2 * D], BF16)
        y8T = sb("y8T", [P, C * S], BF16)
        zf = sb("zf", [P, 2, 2 * D], BF16)
        zg = sb("zg", [P, 2, 2 * D])
        of = sb("of", [P, 2, 2 * D])


        def sems(names):
            return [sem(name) for name in names.split()]

        (ctx_in, x0_in, x_in, x_late_in, gate_in, con_in, att_in, cst_in, l1_in) = sems(
            "ctx_in x0_in x_in x_late_in gate_in con_in att_in cst_in l1_in")
        (set_up, gain_ok, act_tick, dve_tick, pool_tick, dve_own, pool_own) = sems(
            "set_up gain_ok act_tick dve_tick pool_tick dve_own pool_own")
        p0_mm, p0_act, p0_dve = sems("p0_mm p0_act p0_dve")
        (xq_ready, xT_done, xT_copied, scores_done, max_done, exp_done, probT_done, probT_copied, pv_done, x1_done,
         xq1_ready, xT1_done, xT1_copied, logit_done, logit_kept, var_ok, rstd_ok, var1_ok, rstd1_ok, xn_stored) = sems(
            "xq_ready xT_done xT_copied scores_done max_done exp_done probT_done probT_copied pv_done x1_done "
            "xq1_ready xT1_done xT1_copied logit_done logit_kept var_ok rstd_ok var1_ok rstd1_ok xn_stored")
        split_h, split_l = sems("split_h split_l")
        (pairs_ok, rank_done, dif_ok, ex_ok, tok_ok, onerow_ok, onerow_used, slots_done, slots_kept, blocks_kept) = sems(
            "pairs_ok rank_done dif_ok ex_ok tok_ok onerow_ok onerow_used slots_done slots_kept blocks_kept")
        (xz_in, xz_used, xgT_done, xh_ok, xl_ok, h_done, th_ok, gate_ok, g_done, gh_ok, gl_ok, y_done, y_kept) = sems(
            "xz_in xz_used xgT_done xh_ok xl_ok h_done th_ok gate_ok g_done gh_ok gl_ok y_done y_kept")
        (x2_ok, l2_var, l2_rstd, xn2_ok, l3_var, l3_rstd, know_ok, bo_ok, bo_added, s_done, max_ok, e_ok, rec_ok,
         r_done, recT_ok, t_done, pT_ok, v_ok, pvj_done, xt_done, xt_ok, q_done, q_ok, ql_ok, ot_ok, wo_done, x3_ok,
         amax_ok) = sems(
            "x2_ok l2_var l2_rstd xn2_ok l3_var l3_rstd know_ok bo_ok bo_added s_done max_ok e_ok rec_ok r_done "
            "recT_ok t_done pT_ok v_ok pvj_done xt_done xt_ok q_done q_ok ql_ok ot_ok wo_done x3_ok amax_ok")
        (red_ok, red_done, peak_ok, peak_done, scale_ok, wf8_ok, yt_ok, zg_ok, y8_ok, y8_done, y8T_ok, acc_done,
         zf_ok, of_ok) = sems(
            "red_ok red_done peak_ok peak_done scale_ok wf8_ok yt_ok zg_ok y8_ok y8_done y8T_ok acc_done zf_ok "
            "of_ok")
        chunk_in = [sem(f"chunk_in{k}") for k in range(STAGES)]
        gathered = [sem(f"gathered{k}") for k in range(2)]
        y_stored = [sem(f"y_stored{k}") for k in range(2)]
        y_here = [sem(f"y_here{k}") for k in range(2)]
        stored = [sem(f"stored{k}") for k in range(2)]

        def ahead_of(i, k, n):
            return i + (k + n) // 2, (k + n) % 2

        def heads_of(j):
            return [(c, k, 2 * NB * c + 2 * j + k) for c in range(C) for k in range(2)]

        def group_at(b):
            return not isinstance(b, int) or 0 <= b + LEAD < GROUPS

        def batch(b, n):
            return not isinstance(b, int) or 0 <= b + n < B

        def has(b, u, n):
            return not isinstance(b, int) or 0 <= 2 * b + u + n < TILES

        IN_CTX, IN_CON, IN_ATT, IN_CST = 16 * 3, 16 * 4, 16 * 4, 16 * 6

        block = ctx.enter_context(nc.Block())

        P0 = []
        for h in range(2):
            P0 += [("kt0", m, h) for m in range(C)] + [("kq", m, h) for m in range(C)] + [("bqk", 0, h)]
            P0 += [("v0", b, 0) for b in (range(2), range(2, B))[h]]
        CUT = [0, 7, 9, 12, len(P0)]
        P1 = [("kt1", m, h) for m in range(C) for h in range(2)] + [("v1", b, 0) for b in range(B)]
        BY = {"kt0": "act", "kq": "dve", "bqk": "act", "v0": "dve", "kt1": "act", "v1": "act"}

        def evacuated(n):
            items = P0 + P1
            who = BY[items[n][0]]
            return who, sum(BY[it[0]] == who for it in items[:n + 1])

        def p0_number(n):
            return 6 + n % 2 if CUT[1] <= n < len(P0) else 4 + n % 4

        def p0_bank(n):
            return bank[p0_number(n)]

        @block.sync
        def _(sp):
            xv = x.rearrange("(b p u) n -> p b (u n)", p=P, u=U)
            x4 = x_sb[:].rearrange("p (b n) -> p b n", b=B)
            sp.dma_start(ctxT_sb[:], ctxT).then_inc(ctx_in, 16)
            sp.dma_start(x4[:, 0:1, :], xv[:, 0:1, :]).then_inc(x0_in, 16)
            sp.dma_start(x4[:, 1:4, :], xv[:, 1:4, :]).then_inc(x_in, 16)
            sp.dma_start(gate_sb[:, :, 0:E_ALL], gateT).then_inc(gate_in, 16)
            sp.dma_start(gbias_sb[:], gbias.partition_broadcast(P)).then_inc(gate_in, 16)

            def group(m):
                for k in range(STAGES):
                    wait(sp, split_l, STAGES * (m - 1) + k + 1)
                    sp.dma_start(stage[:, k, :], wmoe[:, cols(STAGES * m + k, CHUNK)]).then_inc(chunk_in[k], 16)

            def store_xn(b):
                wait(sp, xq1_ready, b + 1)
                sp.dma_start(xn_d.rearrange("(b p u) n -> b p (u n)", p=P, u=U)[
                    b if isinstance(b, int) else bass.ds(b, 1)], xq1[:]).then_inc(xn_stored, 16)

            late = [(wk1_sb[:], wk1), (wv1_sb[:], wv1), (bv1_sb[0:1, :], bv1), (bk1_sb[:], bk1)]
            group(0)
            sp.dma_start(x4[:, 4:B, :], xv[:, 4:B, :]).then_inc(x_late_in, 16)
            for dst, src in late:
                sp.dma_start(dst, src).then_inc(con_in, 16)
            for m in range(1, LEAD + 1):
                group(m)
            store_xn(0)
            with sp.Fori(LEAD + 1, GROUPS) as m:
                group(m)
                store_xn(m - LEAD)
            with sp.Fori(GROUPS - LEAD, B) as b:
                store_xn(b)
            sp.wait_ge(xn_stored, 16 * B)
            sp.wait_ge(pv_done, B)
            for dst, src in ((wq1_sb, wq1), (bq1_sb, bq1), (wo1_sb, wo1), (wf_sb, wfT)):
                sp.dma_start(dst[:], src).then_inc(l1_in, 16)
            sp.dma_start(bo1_sb[:], bo1.partition_broadcast(P)).then_inc(l1_in, 16)
            sp.dma_start(bf_sb[:], bf.partition_broadcast(P)).then_inc(l1_in, 16)
            xn_b = xn_d.rearrange("(b p u) n -> b p (u n)", p=P, u=U)

            def load_xz(b):
                wait(sp, xz_used, b)
                sp.dma_start(xz[:], xn_b[b if isinstance(b, int) else bass.ds(b, 1)]).then_inc(xz_in, 16)

            def store_y(i):
                for k in range(2):
                    wait(sp, y_kept, 2 * i + k + 1)
                    rows = cols(2 * i + k, P)
                    sp.dma_start(y_d[rows, :], y_sb[:, k, :]).then_inc(y_stored[k], 16)

            store_y(0)
            load_xz(0)
            with sp.Fori(1, B) as i:
                store_y(i)
                load_xz(i)
            with sp.Fori(B, BLOCKS // 2) as i:
                store_y(i)
            out_b = out.rearrange("(b p u) n -> p b (u n)", p=P, u=U)

            def store(i):
                for k in range(2):
                    b = 2 * i + k
                    wait(sp, of_ok, b + 1)
                    sp.dma_start(out_b[:, slice(b, b + 1) if isinstance(b, int) else bass.ds(b, 1), :],
                                 of[:, k:k + 1, :]).then_inc(stored[k], 16)

            with sp.Fori(0, B // 2) as i:
                store(i)
            for k in range(2):
                sp.wait_ge(stored[k], 16 * (B // 2))

        @block.gpsimd
        def _(pool):
            pool.dma_start(ident[:], c_ident).then_inc(cst_in, 16)
            pool.dma_start(gains_sb[:], gains.partition_broadcast(P)).then_inc(cst_in, 16)
            pool.dma_start(tri[:], c_tri).then_inc(cst_in, 16)
            pool.dma_start(count[:], c_count).then_inc(cst_in, 16)
            pool.dma_start(token[:], c_token).then_inc(cst_in, 16)
            pool.dma_start(kmask[:], c_head).then_inc(cst_in, 16)
            pool.memset(half[:], -0.5)
            pool.memset(gate_sb[:, :, E_ALL:P], 0.0)
            pool.memset(ones[:], 1.0).then_inc(set_up, 1)
            pool.wait_ge(set_up, 1)

            def root(var_sem, var_t, rstd_t, out_sem, b):
                wait_apart(pool, var_sem, b + 1, pool_tick)
                pool.tensor_tensor(rstd_t[:], var_t[:], half[:], ALU.pow).then_inc(out_sem, 1)

            def low(m, k):
                wait_apart(pool, split_h, STAGES * m + k + 1, pool_tick)
                c = cols(STAGES * m + k, CHUNK)
                pool.tensor_tensor(wl[:, c], stage[:, k, :], wh[:, c], ALU.subtract).then_inc(split_l, 1)

            def step(b):
                if batch(b, 1):
                    root(var1_ok, var1, rstd1, rstd1_ok, b + 1)
                if group_at(b):
                    for k in range(4):
                        low(b + LEAD, k)
                if batch(b, 4):
                    root(var_ok, var, rstd, rstd_ok, b + 4)

            step(-4)
            step(-3)
            for b in range(-2, 1):
                step(b)
            with pool.Fori(1, B - 4) as b:
                step(b)
            for b in range(B - 4, B):
                step(b)
            pool.wait_ge(slots_kept, 1)
            own = Chain(pool, pool_own, pool_tick)

            def gather(i):
                for k in range(2):
                    wait_apart(pool, gathered[k], 16 * i, pool_tick)
                    own.mark(pool.tensor_copy(slot_now[:, k:k + 1], slot_i[:, cols(2 * i + k, 1)]))
                    own.settle_apart()
                    wait_apart(pool, xgT_done, 2 * i + k - 1, pool_tick)
                    pool.indirect_dma_start(xg[:, k, :], None, xn_d, bass.IndirectOffsetOnAxis(
                        ap=slot_now[:, k:k + 1], axis=0)).then_inc(gathered[k], 16)

            gather(0)
            own.loop(1, BLOCKS // 2, 2, gather)
            for k in range(2):
                pool.wait_ge(y_stored[k], 16 * (BLOCKS // 2))
            pool.wait_ge(l1_in, 16 * 6)

            def fetch(b, u):
                for k in range(2):
                    wait_apart(pool, y_here[u], 32 * b, pool_tick)
                    own.mark(pool.tensor_copy(pos_now[:, 2 * u + k:2 * u + k + 1],
                                              pos_i[:, cols((2 * b + u) + k * TILES, 1)]))
                own.settle_apart()
                wait_apart(pool, x2_ok, 2 * b + u - 1, pool_tick)
                for k in range(2):
                    pool.indirect_dma_start(yg[:, 2 * u + k, :], None, y_d, bass.IndirectOffsetOnAxis(
                        ap=pos_now[:, 2 * u + k:2 * u + k + 1], axis=0)).then_inc(y_here[u], 16)

            def root1(var_sem, var_t, rstd_t, out_sem, b, u):
                wait_apart(pool, var_sem, 2 * b + u + 1, pool_tick)
                pool.tensor_tensor(rstd_t[:, 0:1], var_t[:, 0:1], half[:, 0:1], ALU.pow).then_inc(out_sem, 1)

            def keys(b):
                wait_apart(pool, s_done, 8 * b, pool_tick)
                own.mark(pool.tensor_copy(kpart[:, 0].bitcast(F32R), kt1[:, cols(b, C * LK)]))
                own.settle_apart()
                own.mark(pool.tensor_tensor(kpart[:, 1], kt1[:, cols(b, C * LK)], kpart[:, 0], ALU.subtract))
                own.settle()
                for k in range(2):
                    ins = pool.tensor_tensor(know[:, :, k, :], kpart[:].rearrange("p s (c k) -> p (s c) k", c=C),
                                             kmask[:, k:k + 1].unsqueeze(2).to_broadcast([P, 2 * C, LK]), ALU.mult)
                ins.then_inc(know_ok, 1)

            def values_of(b):
                wait_apart(pool, pvj_done, 8 * b, pool_tick)
                dst = bass.AP(tensor=vnow[:].tensor, offset=vnow[:].offset,
                              ap=[vnow[:].ap[0], [HEADS // C * P, C], [P + DK, HEADS // C], [1, DK]])
                pool.tensor_copy(dst, v1[:, cols(b, D)].rearrange("p (c h d) -> p c h d", c=C, d=DK)).then_inc(v_ok, 1)

            def slot(b, u):
                if u == 1 and has(b, u, 1):
                    keys(b + 1)
                if has(b, u, 4):
                    fetch(*ahead_of(b, u, 4))
                if has(b, u, 2):
                    nb_, nu = ahead_of(b, u, 2)
                    wait_apart(pool, xn2_ok, 2 * nb_ + nu + 1, pool_tick)
                    t = cols(2 * nb_ + nu, D)
                    pool.tensor_tensor(x_sb[:, t], x_sb[:, t], bo1g[:], ALU.add).then_inc(bo_added, 1)
                if has(b, u, 3):
                    root1(l2_var, var, rstd, l2_rstd, *ahead_of(b, u, 3))
                if has(b, u, -1):
                    root1(l3_var, var1, rstd1, l3_rstd, *ahead_of(b, u, -1))
                if u == 1 and has(b, u, 1):
                    values_of(b + 1)

            def pair(i):
                slot(i, 0)
                slot(i, 1)

            fetch(0, 0)
            own.mark(pool.memset(vnow[:], 0.0))
            own.settle()
            pool.wait_ge(bo_ok, 1)
            slot(-2, 1)
            pair(-1)
            pair(0)
            own.loop(1, B - 2, 6, pair)
            pair(B - 2)
            pair(B - 1)
            slot(B, 0)

            def round_off(b, k):
                wait_apart(pool, yt_ok, b + 1, pool_tick)
                wait_apart(pool, y8_done, b, pool_tick)
                pool.tensor_tensor(y8[:], yt[:, k, :], ym[:, k, :], ALU.subtract).then_inc(y8_ok, 1)

            def add_ffn(b, k):
                wait_apart(pool, zg_ok, b + 1, pool_tick)
                wait_apart(pool, stored[k], 8 * (b - k), pool_tick)
                pool.tensor_tensor(of[:, k, :], zg[:, k, :], x_sb[:, cols(b, U * D)], ALU.add).then_inc(of_ok, 1)

            def pair(i):
                for k in range(2):
                    round_off(2 * i + (k + 2), k)
                    add_ffn(2 * i + k, k)

            round_off(0, 0)
            round_off(1, 1)
            pair(0)
            with pool.Fori(1, B // 2 - 1) as i:
                pair(i)
            for k in range(2):
                add_ffn(B - 2 + k, k)

        @block.scalar
        def _(act):
            for dst, src in ((wk0_sb, wk0), (bk0_sb, bk0)):
                act.dma_start(dst[:], src).then_inc(ctx_in, 16)
            for dst, src in ((wq0_sb, wq0T), (bq0_sb, bq0), (wv0_sb, wv0)):
                act.dma_start(dst[:], src).then_inc(att_in, 16)
            act.dma_start(bv0_sb[:], bv0.partition_broadcast(P)).then_inc(att_in, 16)
            act.wait_ge(ctx_in, IN_CTX)

            def high(m, k):
                wait(act, chunk_in[k], 16 * (m + 1))
                if not isinstance(m, int):
                    act.sem_inc(act_tick, 1)
                nc.scalar.activation(wh[:, cols(STAGES * m + k, CHUNK)], stage[:, k, :], ACT.Copy).then_inc(split_h, 1)

            def empty(cut):
                for n, (what, m, h) in list(enumerate(P0))[CUT[cut]:CUT[cut + 1]]:
                    if BY[what] != "act":
                        continue
                    act.wait_ge(p0_mm, n + 1)
                    if what == "kt0":
                        nc.scalar.activation(kt0[:, m, :], p0_bank(n)[:, 0:HB], ACT.Identity,
                                             bias=bk0_sb[:, m:m + 1]).then_inc(p0_act, 1)
                    else:
                        nc.scalar.activation(bqk[0:1, h * HB:(h + 1) * HB], p0_bank(n)[0:1, 0:HB],
                                             ACT.Copy).then_inc(p0_act, 1)

            def copy_xT(b):
                wait(act, xT_done, b + 1)
                wait_apart(act, scores_done, b, act_tick)
                nc.scalar.activation(xT[:], bank[0][:], ACT.Copy).then_inc(xT_copied, 1)

            def exp_of(b):
                wait(act, max_done, b + 1)
                wait_apart(act, probT_done, b, act_tick)
                for u in range(U):
                    ins = nc.scalar.activation(prob[:, u * LK:(u + 1) * LK], bank[1][:, u * LK:(u + 1) * LK], ACT.Exp,
                                               bias=negmax[:, u:u + 1], accum_out=psum[:, u:u + 1])
                ins.then_inc(exp_done, 1)

            def copy_probT(b):
                wait(act, probT_done, b + 1)
                wait_apart(act, pv_done, b, act_tick)
                nc.scalar.activation(probT[:], bank[2][0:LK, 0:S], ACT.Copy).then_inc(probT_copied, 1)

            def copy_xT1(b):
                wait(act, xT1_done, b + 1)
                wait_apart(act, logit_done, b, act_tick)
                nc.scalar.activation(xT1[:], bank[4][:], ACT.Copy).then_inc(xT1_copied, 1)

            def step(b):
                if group_at(b):
                    high(b + LEAD, 0)
                if batch(b, 0):
                    copy_xT1(b)
                if batch(b, 2):
                    exp_of(b + 2)
                if group_at(b):
                    high(b + LEAD, 1)
                if batch(b, 2):
                    copy_probT(b + 2)
                if group_at(b):
                    high(b + LEAD, 2)
                if batch(b, 3):
                    copy_xT(b + 3)
                if group_at(b):
                    high(b + LEAD, 3)

            empty(0)
            act.wait_ge(cst_in, IN_CST)
            nc.scalar.activation(gain[:], gains_sb[:], ACT.Tanh).then_inc(gain_ok, 1)
            nc.scalar.activation(identb[:], ident[:], ACT.Copy)
            step(-4)
            step(-3)
            for b in range(-2, 1):
                step(b)
                empty(b + 3)
            with act.Fori(1, B - 4) as b:
                step(b)
            for b in range(B - 4, B):
                step(b)

            act.wait_ge(con_in, IN_CON)
            act.wait_ge(pv_done, B)
            for n, (what, m, h) in enumerate(P1, len(P0)):
                act.wait_ge(p0_mm, n + 1)
                if what == "kt1":
                    half_of = kt1[:].rearrange("p (b c k) -> p b c k", b=B, c=C)[:, h * B // 2:(h + 1) * B // 2, m, :]
                    nc.scalar.activation(half_of,
                                         p0_bank(n)[:, 0:HB].rearrange("p (b k) -> p b k", k=LK), ACT.Identity,
                                         bias=bk1_sb[:, m:m + 1]).then_inc(p0_act, 1)
                else:
                    nc.scalar.activation(v1[:, m * D:(m + 1) * D], p0_bank(n)[0:LK, 0:D], ACT.Copy).then_inc(p0_act, 1)
                if n == len(P0) + B:
                    act.wait_ge(dif_ok, 1)
                    nc.scalar.activation(ex[:], dif[:], ACT.Exp).then_inc(ex_ok, 1)

            def xh_of(i, k):
                wait(act, xgT_done, 2 * i + k + 1)
                wait(act, h_done, 2 * i + k - 1)
                nc.scalar.activation(xh[:, k, :], bank[k][:, 0:D], ACT.Copy).then_inc(xh_ok, 1)

            def th_of(i, k):
                wait(act, h_done, 2 * i + k + 1)
                wait(act, gate_ok, 2 * i + k)
                nc.scalar.activation(th[:], bank[2 + k][:], ACT.Tanh, scale=0.5).then_inc(th_ok, 1)

            def slot(i, k, last=BLOCKS):
                wait(act, g_done, 2 * i + k + 1)
                wait(act, y_done, 2 * i + k - 1)
                nc.scalar.activation(gh[:, k, :], bank[4 + k][:], ACT.Copy).then_inc(gh_ok, 1)
                if last > 1:
                    th_of(*ahead_of(i, k, 1))
                if last > 2:
                    xh_of(*ahead_of(i, k, 2))
                wait(act, y_done, 2 * i + k + 1)
                wait(act, y_stored[k], 16 * i)
                nc.scalar.activation(y_sb[:, k, :], bank[6 + k][:, 0:D], ACT.Copy).then_inc(y_kept, 1)

            xh_of(0, 0)
            xh_of(0, 1)
            th_of(0, 0)
            slot(0, 0)
            slot(0, 1)
            with act.Fori(1, BLOCKS // 2 - 1) as i:
                slot(i, 0)
                slot(i, 1)
            slot(BLOCKS // 2 - 1, 0, 2)
            slot(BLOCKS // 2 - 1, 1, 1)

            def exp_of(b, u, j):
                n = 8 * b + 4 * u + j
                wait(act, max_ok, n + 1)
                wait(act, t_done, n - 3)
                for m in range(HG):
                    h, head = HG * j + m, heads_of(j)[m][2]
                    ins = nc.scalar.activation(sc[:, j, m * LK:(m + 1) * LK], bank[j][:, m * LK:(m + 1) * LK], ACT.Exp,
                                               bias=nm[:, h:h + 1], accum_out=ssum[:, u, head:head + 1])
                ins.then_inc(e_ok, 1)

            def copy_pT(b, u, j):
                wait(act, t_done, 8 * b + 4 * u + j + 1)
                wait(act, pvj_done, 8 * b + 4 * u + j - 3)
                nc.scalar.activation(pT[:, j, :], bank[4 + j % 2][0:LK, :], ACT.Copy).then_inc(pT_ok, 1)

            def copy_recT(b, u):
                wait(act, r_done, 2 * b + u + 1)
                wait(act, ot_ok, 2 * b + u)
                nc.scalar.activation(recT[:], bank[7][:, 0:D], ACT.Copy).then_inc(recT_ok, 1)

            def copy_xT2(b, u):
                wait(act, xt_done, 2 * b + u + 1)
                wait(act, q_done, 2 * b + u)
                nc.scalar.activation(xT2[:], bank[7][:, 0:D], ACT.Copy).then_inc(xt_ok, 1)

            def copy_q(b, u):
                wait(act, q_done, 2 * b + u + 1)
                wait(act, s_done, 8 * b + 4 * u - 4)
                for m in range(C):
                    ins = nc.scalar.activation(qh[:, u, m * P:(m + 1) * P], bank[7][:, m * P:(m + 1) * P], ACT.Identity,
                                               bias=bq1_sb[:, m:m + 1])
                ins.then_inc(q_ok, 1)

            def slot(b, u):
                if has(b, u, 2):
                    copy_xT2(*ahead_of(b, u, 2))
                if has(b, u, 0):
                    copy_pT(b, u, 0)
                    copy_pT(b, u, 1)
                if has(b, u, 2):
                    copy_q(*ahead_of(b, u, 2))
                if has(b, u, 0):
                    exp_of(b, u, 3)
                    copy_pT(b, u, 2)
                    copy_pT(b, u, 3)
                    copy_recT(b, u)
                if has(b, u, 1):
                    exp_of(*ahead_of(b, u, 1), 0)
                    exp_of(*ahead_of(b, u, 1), 1)
                    exp_of(*ahead_of(b, u, 1), 2)

            act.wait_ge(l1_in, 16 * 6)
            def pair(i):
                slot(i, 0)
                slot(i, 1)

            slot(-2, 1)
            pair(-1)
            pair(0)
            with act.Fori(1, B - 2) as i:
                pair(i)
            pair(B - 2)
            pair(B - 1)
            slot(B, 0)

            def copy_y8T(b):
                wait(act, y8_done, b + 1)
                wait(act, acc_done, b)
                nc.scalar.activation(y8T[:], bank[2][:].bitcast(BF16)[:, 0:C * S], ACT.Copy).then_inc(y8T_ok, 1)

            def times_gain(b, k):
                wait(act, zf_ok, b + 1)
                wait(act, of_ok, b - 1)
                nc.scalar.activation(zg[:, k, :], zf[:, k, :], ACT.Copy, scale=gain[:, 3:4]).then_inc(zg_ok, 1)

            def step(i, k, after=True):
                if after:
                    copy_y8T(2 * i + k)
                if not isinstance(i, int) or i or k:
                    times_gain(2 * i + (k - 1), 1 - k)

            for i in range(2):
                step(i, 0)
                step(i, 1)
            with act.Fori(2, B // 2) as i:
                step(i, 0)
                step(i, 1)
            step(B // 2, 0, after=False)

        @block.vector
        def _(dve):
            own = Chain(dve, dve_own, dve_tick)

            def norm_stats(src, stat_t, mean_t, var_t, out_sem):
                for u in range(U):
                    ins = dve.bn_stats(stat_t[:, u, :], src(u))
                own.mark(ins)
                own.settle_apart()
                for u in range(U):
                    ins = dve.bn_aggr(mean_t[:, u, :], stat_t[:, u, :])
                own.mark(ins)
                own.settle()
                dve.tensor_scalar(var_t[:], mean_t[:, :, 1], EPS, None, ALU.add).then_inc(out_sem, 1)

            def tile_of(b):
                return lambda u: x_sb[:, cols(2 * b + u, D)]

            def ahead_norm(b):
                wait(dve, rstd_ok, b + 1)
                wait_apart(dve, xT_done, b, dve_tick)
                for u in range(U):
                    ins = dve.tensor_scalar(xq[:, u * D:(u + 1) * D], tile_of(b)(u), mean[:, u, 0:1], rstd[:, u:u + 1],
                                            ALU.subtract, ALU.mult)
                ins.then_inc(xq_ready, 1)

            def ahead_max(b):
                wait(dve, scores_done, b + 1)
                wait_apart(dve, exp_done, b, dve_tick)
                dve.tensor_reduce(negmax[:], bank[1][:, 0:U * LK].rearrange("p (u k) -> p u k", u=U), AX, ALU.max,
                                  negate=True).then_inc(max_done, 1)

            def sums(b):
                wait(dve, exp_done, b + 1)
                own.mark(dve.reciprocal(rsum[:], psum[:]))
                own.settle()
                own.mark(dve.tensor_scalar(rsumg[:], rsum[:], gain[:, 0:1], None, ALU.mult))
                own.settle()

            def add_x1(b):
                wait(dve, pv_done, b + 1)
                if not isinstance(b, int):
                    dve.sem_inc(dve_tick, 1)
                for u in range(U):
                    ins = dve.scalar_tensor_tensor(tile_of(b)(u), bank[3][:, u * D:(u + 1) * D], rsumg[:, u:u + 1],
                                                   tile_of(b)(u), ALU.mult, ALU.add)
                ins.then_inc(x1_done, 1)
                wait_apart(dve, x1_done, b + 1, dve_tick)
                norm_stats(tile_of(b), stat1, mean1, var1, var1_ok)

            def norm1(b):
                wait(dve, rstd1_ok, b + 1)
                wait(dve, xn_stored, 16 * b)
                wait_apart(dve, xT1_done, b, dve_tick)
                for u in range(U):
                    ins = dve.tensor_scalar(xq1[:, u * D:(u + 1) * D], tile_of(b)(u), mean1[:, u, 0:1],
                                            rstd1[:, u:u + 1], ALU.subtract, ALU.mult)
                ins.then_inc(xq1_ready, 1)

            def logits_of(b):
                wait_apart(dve, logit_done, b + 1, dve_tick)
                dve.tensor_tensor(logit[:, cols(b, U * E_ALL)].rearrange("p (u e) -> p u e", u=U),
                                  bank[5][:, 0:U * P].rearrange("p (u e) -> p u e", u=U)[:, :, 0:E_ALL],
                                  gbias_sb[:].rearrange("p (u e) -> p u e", u=U), ALU.add).then_inc(logit_kept, 1)

            def step(b):
                if batch(b, 1):
                    add_x1(b + 1)
                if batch(b, 2):
                    ahead_max(b + 2)
                if batch(b, 0):
                    logits_of(b)
                if batch(b, 3):
                    ahead_norm(b + 3)
                if batch(b, 1):
                    norm1(b + 1)
                if batch(b, 2):
                    sums(b + 2)
                if batch(b, 4):
                    norm_stats(tile_of(b + 4), stat, mean, var, var_ok)

            dve.wait_ge(x0_in, 16)
            step(-4)

            def empty(cut):
                for n, (what, m, h) in list(enumerate(P0))[CUT[cut]:CUT[cut + 1]]:
                    if BY[what] != "dve":
                        continue
                    dve.wait_ge(p0_mm, n + 1)
                    if what == "kq":
                        half_of = kq[:].rearrange("p (b c k) -> p b c k", b=B, c=C)[:, h * B // 2:(h + 1) * B // 2, m, :]
                        dve.tensor_copy(half_of,
                                        p0_bank(n)[:, 0:HB].rearrange("p (b k) -> p b k", k=LK)).then_inc(p0_dve, 1)
                    else:
                        dve.tensor_tensor(v0[:, m * D:(m + 1) * D], p0_bank(n)[0:LK, 0:D], bv0_sb[0:LK, :],
                                          ALU.add).then_inc(p0_dve, 1)

            dve.wait_ge(att_in, IN_ATT)
            empty(0)
            dve.wait_ge(x_in, 16)
            dve.wait_ge(gain_ok, 1)
            step(-3)
            for b in range(-2, 1):
                if b == 0:
                    dve.wait_ge(x_late_in, 16)
                    dve.wait_ge(gate_in, 32)
                step(b)
                empty(b + 3)
            own.loop(1, B - 4, 6, step)
            for b in range(B - 4, B):
                step(b)

            def then(ins):
                own.mark(ins)
                own.settle()

            def wide(ap, n):
                return ap.unsqueeze(2).to_broadcast([P, ap.shape[1], n])

            def over(ap, n):
                return ap.unsqueeze(1).to_broadcast([P, n, ap.shape[1]])

            dve.wait_ge(logit_kept, B)
            lg = logit[:].rearrange("p (t e) -> p t e", e=E_ALL)
            numbers = over(count[:, 0:E_ALL], TILES)
            then(dve.tensor_reduce(top[:, 0, :], lg, AX, ALU.max))
            for k in range(2):
                src = lg if k == 0 else left[:]
                then(dve.tensor_tensor(eq[:], src, wide(top[:, k, :], E_ALL), ALU.is_equal))
                then(dve.scalar_tensor_tensor(cand[:], eq[:], -64.0, numbers, ALU.mult, ALU.add))
                then(dve.tensor_reduce(pick[:], cand[:], AX, ALU.min))
                then(dve.tensor_tensor(hot[:, k], cand[:], wide(pick[:], E_ALL), ALU.is_equal))
                if k == 0:
                    then(dve.scalar_tensor_tensor(left[:], hot[:, 0], -3.0e38, lg, ALU.mult, ALU.add))
                    then(dve.tensor_reduce(top[:, 1, :], left[:], AX, ALU.max))
                    dve.tensor_tensor(dif[:], top[:, 1, :], top[:, 0, :], ALU.subtract).then_inc(dif_ok, 1)
            dve.tensor_tensor(pairs[:], hot[:, 0, :, 0:E_FFN], hot[:, 1, :, 0:E_FFN], ALU.add).then_inc(pairs_ok, 1)
            then(dve.tensor_reduce(valid[:].rearrange("p k t -> p (k t)"),
                                   hot[:].rearrange("p k t e -> p (k t) e")[:, :, 0:E_FFN], AX, ALU.add))
            dve.wait_ge(xn_stored, 16 * B)
            dve.wait_ge(split_l, CHUNKS)
            for q in pre:
                ins = dve.memset(q[:, 0:pad, :], 0.0)
            for q in nb:
                ins = dve.memset(q[:, 0:4], 0.0)
            then(ins)
            dve.wait_ge(rank_done, 1)
            then(dve.tensor_copy(pre[0][:, pad:, :], bank[0][:, P:2 * P].rearrange("p (t e) -> p t e", e=E_FFN)))
            a, z = 0, 1
            for n in (1, 2, 4, 8):
                then(dve.tensor_tensor(pre[z][:, pad:, :], pre[a][:, pad:, :], pre[a][:, pad - n:pad + TILES - n, :],
                                       ALU.add))
                a, z = z, a
            upto = pre[a]
            then(dve.tensor_scalar(cnt_i[:], upto[:, pad + TILES - 1, :], P - 1.0, None, ALU.add))
            then(dve.tensor_scalar(nb_i[:], cnt_i[:], 7, None, ALU.arith_shift_right))
            then(dve.tensor_copy(nb[0][:, 4:], nb_i[:]))
            then(dve.tensor_scalar(nbk[:], nb[0][:, 4:], float(P), None, ALU.mult))
            a, z = 0, 1
            for n in (1, 2, 4):
                then(dve.tensor_tensor(nb[z][:, 4:], nb[a][:, 4:], nb[a][:, 4 - n:4 + E_FFN - n], ALU.add))
                a, z = z, a
            blocks = nb[a]
            then(dve.scalar_tensor_tensor(nbk[:], blocks[:, 4:], float(P), nbk[:], ALU.mult, ALU.subtract))
            then(dve.tensor_tensor(place[:], bank[0][:, 0:P].rearrange("p (t e) -> p t e", e=E_FFN),
                                   over(nbk[:], TILES), ALU.add))
            then(dve.tensor_tensor(place[:], place[:], upto[:, pad - 1:pad + TILES - 1, :], ALU.add))
            for k in range(2):
                ins = dve.tensor_tensor(prod[:, k], hot[:, k, :, 0:E_FFN], place[:], ALU.mult)
            then(ins)
            then(dve.tensor_reduce(pos[:], prod[:].rearrange("p k t e -> p (k t) e"), AX, ALU.add))
            then(dve.tensor_copy(pos_i[:], pos[:]))
            dve.tensor_scalar(row_i[:], pos_i[:], P - 1, None, ALU.bitwise_and)
            then(dve.tensor_scalar(col_i[:], pos_i[:], 7, None, ALU.arith_shift_right))
            dve.tensor_copy(row[:], row_i[:])
            then(dve.tensor_copy(col[:], col_i[:]))
            then(dve.scalar_tensor_tensor(col[:], col[:], 1.0, valid[:].rearrange("p k t -> p (k t)"), ALU.add, ALU.mult))
            then(dve.tensor_scalar(col[:], col[:], -1.0, None, ALU.add))
            then(dve.tensor_tensor(onecol[:], over(count[:, 0:BLOCKS], 2 * TILES), wide(col[:], BLOCKS), ALU.is_equal))
            dve.tensor_tensor(tokcol[:], onecol[:], wide(token[:], BLOCKS), ALU.mult).then_inc(tok_ok, 1)
            for n in range(4):
                wait(dve, onerow_used, n - 1)
                dve.tensor_tensor(onerow[:, n % 2], over(count[:], 8), wide(row[:, 8 * n:8 * n + 8], P),
                                  ALU.is_equal).then_inc(onerow_ok, 1)
            then(dve.tensor_tensor(cmp[:], over(blocks[:, 4:3 + E_FFN], BLOCKS + 2), wide(count[:, 0:BLOCKS + 2], E_FFN - 1),
                                   ALU.is_le))
            then(dve.tensor_reduce(blk[:], cmp[:], AX, ALU.add))
            for k in range(3):
                ins = dve.scalar_tensor_tensor(blk_i[:] if k == 2 else blks[:, k, :], blk[:, k + 1:k + BLOCKS:2],
                                               float(E_FFN ** (k + 1)), blks[:, k - 1, :] if k else blk[:, 0:BLOCKS:2],
                                               ALU.mult, ALU.add)
                if k < 2:
                    then(ins)
            ins.then_inc(blocks_kept, 1)
            dve.wait_ge(slots_done, 1)
            dve.tensor_copy(slot_i[:], bank[1][:, 0:BLOCKS]).then_inc(slots_kept, 1)
            dve.wait_ge(ex_ok, 1)
            then(dve.tensor_scalar(dif[:], ex[:], 1.0, None, ALU.add))
            then(dve.reciprocal(wgt[:, 0, :], dif[:]))
            then(dve.tensor_tensor(wgt[:, 1, :], wgt[:, 0, :], ex[:], ALU.mult))
            then(dve.tensor_tensor(wval[:], wgt[:], valid[:], ALU.mult))
            then(dve.tensor_scalar(cw[:], wval[:].rearrange("p k t -> p (k t)"), gain[:, 1:2], 0.5, ALU.mult, ALU.mult))
            then(dve.tensor_tensor(wgt[:], wgt[:], wval[:], ALU.subtract))
            then(dve.tensor_tensor(cz[:], wgt[:, 0, :], wgt[:, 1, :], ALU.add))
            then(dve.tensor_scalar(cz[:], cz[:], gain[:, 1:2], None, ALU.mult))

            def xl_of(i, k):
                wait(dve, xh_ok, 2 * i + k + 1)
                dve.tensor_tensor(xl[:, k, :], bank[k][:, 0:D], xh[:, k, :], ALU.subtract).then_inc(xl_ok, 1)

            def gate_of(i, k):
                wait(dve, th_ok, 2 * i + k + 1)
                wait(dve, g_done, 2 * i + k - 1)
                dve.scalar_tensor_tensor(gate[:, k, :], th[:], 1.0, bank[2 + k][:], ALU.add, ALU.mult).then_inc(gate_ok, 1)

            def slot(i, k, last=BLOCKS):
                wait(dve, gh_ok, 2 * i + k + 1)
                dve.tensor_tensor(gl[:, k, :], bank[4 + k][:], gh[:, k, :], ALU.subtract).then_inc(gl_ok, 1)
                if last > 1:
                    gate_of(*ahead_of(i, k, 1))
                if last > 2:
                    xl_of(*ahead_of(i, k, 2))

            def pair(i):
                slot(i, 0)
                slot(i, 1)

            def pair_xz(i):
                for k in range(2):
                    slot(i, k)
                    if k == 0:
                        wait_apart(dve, xz_in, 16 * i, dve_tick)
                    t = 2 * i + (k - 2)
                    ins = dve.scalar_tensor_tensor(x_sb[:, cols(t, D)], xz[:, k * D:(k + 1) * D], cz[:, cols(t, 1)],
                                                   x_sb[:, cols(t, D)], ALU.mult, ALU.add)
                ins.then_inc(xz_used, 1)

            xl_of(0, 0)
            xl_of(0, 1)
            gate_of(0, 0)
            pair(0)
            with dve.Fori(1, B + 1) as i:
                pair_xz(i)
            with dve.Fori(B + 1, BLOCKS // 2 - 1) as i:
                pair(i)
            slot(BLOCKS // 2 - 1, 0, 2)
            slot(BLOCKS // 2 - 1, 1, 1)

            def combine(b, u):
                t = cols(2 * b + u, D)
                wait(dve, y_here[u], 32 * (b + 1))
                for k in range(2):
                    if k or not isinstance(b, int):
                        dve.sem_inc(dve_tick, 1)
                    ins = dve.scalar_tensor_tensor(x_sb[:, t], yg[:, 2 * u + k, :], cw[:, cols((2 * b + u) + k * TILES, 1)],
                                                   x_sb[:, t], ALU.mult, ALU.add)
                    if k == 0:
                        own.mark(ins)
                        own.settle()
                ins.then_inc(x2_ok, 1)

            def stats2(b, u):
                wait_apart(dve, x2_ok, 2 * b + u + 1, dve_tick)
                stats1(x_sb[:, cols(2 * b + u, D)], stat, mean, var, l2_var)

            def stats1(src, stat_t, mean_t, var_t, out_sem):
                own.mark(dve.bn_stats(stat_t[:, 0, :], src))
                own.settle_apart()
                own.mark(dve.bn_aggr(mean_t[:, 0, :], stat_t[:, 0, :]))
                own.settle()
                dve.tensor_scalar(var_t[:, 0:1], mean_t[:, 0, 1:2], EPS, None, ALU.add).then_inc(out_sem, 1)

            def norm2(b, u):
                wait(dve, l2_rstd, 2 * b + u + 1)
                wait_apart(dve, xt_done, 2 * b + u - 1, dve_tick)
                dve.tensor_scalar(xq2[:, u, :], x_sb[:, cols(2 * b + u, D)], mean[:, 0, 0:1], rstd[:, 0:1],
                                  ALU.subtract, ALU.mult).then_inc(xn2_ok, 1)

            def maxima(b, u, j):
                wait(dve, s_done, 8 * b + 4 * u + j + 1)
                dve.tensor_reduce(nm[:, j * HG:(j + 1) * HG], bank[j][:, 0:HG * LK].rearrange("p (h k) -> p h k", k=LK),
                                  AX, ALU.max, negate=True).then_inc(max_ok, 1)

            def add_attention(b, u):
                t = cols(2 * b + u, D)
                wait(dve, wo_done, 2 * b + u + 1)
                wait_apart(dve, bo_added, 2 * b + u + 1, dve_tick)
                dve.scalar_tensor_tensor(x_sb[:, t], bank[7][:, 0:D], gain[:, 2:3], x_sb[:, t],
                                         ALU.mult, ALU.add).then_inc(x3_ok, 1)

            def stats3(b, u):
                wait_apart(dve, x3_ok, 2 * b + u + 1, dve_tick)
                stats1(x_sb[:, cols(2 * b + u, D)], stat1, mean1, var1, l3_var)

            def low_q(b, u):
                wait(dve, q_ok, 2 * b + u + 1)
                wait_apart(dve, s_done, 8 * b + 4 * u - 4, dve_tick)
                for m in range(C):
                    t = slice(m * P, (m + 1) * P)
                    ins = dve.scalar_tensor_tensor(ql[:, u, t], bank[7][:, t], bq1_sb[:, m:m + 1], qh[:, u, t],
                                                   ALU.add, ALU.subtract)
                ins.then_inc(ql_ok, 1)

            def one_over(b, u):
                wait(dve, e_ok, 8 * b + 4 * u + 4)
                wait_apart(dve, r_done, 2 * b + u, dve_tick)
                then(dve.reciprocal(rec1[:], ssum[:, u, :]))
                dve.tensor_copy(rec[:], wide(rec1[:], DK)).then_inc(rec_ok, 1)

            def divide(b, u):
                wait(dve, pvj_done, 8 * b + 4 * u + 4)
                wait_apart(dve, recT_ok, 2 * b + u + 1, dve_tick)
                wait_apart(dve, wo_done, 2 * b + u, dve_tick)
                dve.tensor_tensor(oT[:], bank[6][:, 0:D], recT[:], ALU.mult).then_inc(ot_ok, 1)

            def norm3(b, u):
                t = cols(2 * b + u, D)
                wait_apart(dve, l3_rstd, 2 * b + u + 1, dve_tick)
                own.mark(dve.tensor_scalar(xn_sb[:, t], x_sb[:, t], mean1[:, 0, 0:1], rstd1[:, 0:1],
                                           ALU.subtract, ALU.mult))
                own.settle_apart()
                dve.tensor_reduce(amx[:, cols(2 * b + u, 1)], xn_sb[:, t], AX, ALU.max,
                                  apply_absolute_value=True).then_inc(amax_ok, 1)

            def slot(b, u):
                if has(b, u, -1):
                    divide(*ahead_of(b, u, -1))
                if has(b, u, 3):
                    combine(*ahead_of(b, u, 3))
                if has(b, u, 2):
                    low_q(*ahead_of(b, u, 2))
                if has(b, u, 3):
                    stats2(*ahead_of(b, u, 3))
                if has(b, u, 0):
                    one_over(b, u)
                if has(b, u, -1):
                    add_attention(*ahead_of(b, u, -1))
                if has(b, u, 1):
                    maxima(*ahead_of(b, u, 1), 0)
                if has(b, u, -1):
                    stats3(*ahead_of(b, u, -1))
                if has(b, u, 1):
                    maxima(*ahead_of(b, u, 1), 1)
                if has(b, u, 3):
                    norm2(*ahead_of(b, u, 3))
                if has(b, u, 1):
                    maxima(*ahead_of(b, u, 1), 2)
                if has(b, u, -1):
                    norm3(*ahead_of(b, u, -1))
                if has(b, u, 1):
                    maxima(*ahead_of(b, u, 1), 3)

            def pair(i):
                slot(i, 0)
                slot(i, 1)

            def scale_of(c, src, n):
                dve.tensor_reduce(red[:, c:c + 1], src, AX, ALU.max, apply_absolute_value=True).then_inc(red_ok, 1)
                dve.wait_ge(red_done, n)
                dve.tensor_reduce(peak[0:1, c:c + 1], bank[0][0:1, 0:P], AX, ALU.max).then_inc(peak_ok, 1)
                dve.wait_ge(peak_done, n)
                then(dve.tensor_scalar(red[:, 2 + c:3 + c], bank[1][:, 0:1], 1e-12, None, ALU.max))
                then(dve.reciprocal(red[:, 4 + c:5 + c], red[:, 2 + c:3 + c]))
                own.mark(dve.tensor_scalar(red[:, 6 + c:7 + c], red[:, 4 + c:5 + c], FP8_MAX, FP8_MAX,
                                           ALU.mult, ALU.min))
                own.settle()
                then(dve.reciprocal(red[:, 8 + c:9 + c], red[:, 6 + c:7 + c]))
                dve.sem_inc(scale_ok, 1)

            def to_f8(src, scale, k):
                then(dve.tensor_scalar(yq[:], src, scale, FP8_MAX, ALU.mult, ALU.min))
                then(dve.tensor_scalar(ye[:], yq[:].bitcast(I32), 0x7F800000, None, ALU.bitwise_and))
                then(dve.tensor_scalar(ym[:, k, :], ye[:].bitcast(F32), TINY, MAGIC, ALU.max, ALU.mult))
                return dve.scalar_tensor_tensor(yt[:, k, :], yq[:], -FP8_MAX, ym[:, k, :], ALU.max, ALU.add)

            dve.wait_ge(l1_in, 16 * 6)
            dve.wait_ge(y_done, BLOCKS)
            scale_of(1, wf_sb[:], 1)
            then(to_f8(wf_sb[:], red[:, 7:8], 0))
            dve.tensor_tensor(wf8[:], yt[:, 0, :], ym[:, 0, :], ALU.subtract).then_inc(wf8_ok, 1)
            dve.tensor_scalar(bo1g[:], bo1_sb[:], gain[:, 2:3], None, ALU.mult).then_inc(bo_ok, 1)
            slot(-2, 1)
            pair(-1)
            pair(0)
            own.loop(1, B - 2, 2 * 7, pair)
            pair(B - 2)
            pair(B - 1)
            slot(B, 0)

            dve.wait_ge(amax_ok, TILES)
            scale_of(0, amx[:], 2)
            then(dve.tensor_scalar(red[:, 10:11], red[:, 8:9], red[:, 9:10], None, ALU.mult))

            def quantise(b, k):
                wait_apart(dve, y8_ok, b - 1, dve_tick)
                wait_apart(dve, yt_ok, b, dve_tick)
                to_f8(xn_sb[:, cols(b, U * D)], red[:, 6:7], k).then_inc(yt_ok, 1)

            def finish(b, k):
                wait(dve, acc_done, b + 1)
                wait_apart(dve, of_ok, b - 1, dve_tick)
                dve.scalar_tensor_tensor(zf[:, k, :].rearrange("p (u n) -> p u n", u=U),
                                         bank[4 + k][:].rearrange("p (u n) -> p u n", u=U), red[:, 10:11],
                                         over(bf_sb[:], U), ALU.mult, ALU.add).then_inc(zf_ok, 1)

            def pair(i):
                for k in range(2):
                    quantise(2 * i + (k + 2), k)
                    finish(2 * i + k, k)

            quantise(0, 0)
            quantise(1, 1)
            pair(0)
            own.loop(1, B // 2 - 1, 6, pair)
            finish(B - 2, 0)
            finish(B - 1, 1)

        @block.tensor
        def _(pe):
            def free_bank(n):
                for m in range(n - 1, -1, -1):
                    if p0_number(m) == p0_number(n):
                        who, k = evacuated(m)
                        pe.wait_ge(p0_act if who == "act" else p0_dve, k)
                        break

            pe.wait_ge(ctx_in, IN_CTX)

            def transposes(dst, src):
                for c in range(C):
                    for u in range(U):
                        ins = pe.transpose(dst[:, c * S + u * P:c * S + u * P + P],
                                           src[:, u * D + c * P:u * D + c * P + P], ident[:])
                return ins

            def ahead_xT(b):
                wait(pe, xq_ready, b + 1)
                wait(pe, xT_copied, b)
                transposes(bank[0], xq).then_inc(xT_done, 1)

            def ahead_scores(b):
                wait(pe, xT_copied, b + 1)
                wait(pe, exp_done, b)
                for u in range(U):
                    dst = bank[1][:, u * LK:(u + 1) * LK]
                    for c in range(C):
                        k = slice(b * C * LK + c * LK, b * C * LK + c * LK + LK) if isinstance(b, int) \
                            else bass.ds(b * (C * LK) + c * LK, LK)
                        pe.matmul(dst, xT[:, c * S + u * P:c * S + u * P + P], kq[:, k], start=(c == 0), stop=False)
                    ins = pe.matmul(dst, ones[0:1, :], bqk[0:1, cols(b, LK)], start=False, stop=True)
                ins.then_inc(scores_done, 1)

            def products(cut):
                for n, (what, m, h) in list(enumerate(P0))[CUT[cut]:CUT[cut + 1]]:
                    free_bank(n)
                    hs = slice(h * HB, (h + 1) * HB)
                    if what == "kt0":
                        ins = pe.matmul(p0_bank(n)[:, 0:HB], wk0_sb[:, m * P:(m + 1) * P], ctxT_sb[:, hs], start=True,
                                        stop=True)
                    if what == "kq" and n == 2:
                        pe.wait_ge(att_in, IN_ATT)
                    if what in ("kq", "bqk"):
                        kt0_there = max(k for k, it in enumerate(P0) if it[0] == "kt0" and it[2] == h)
                        pe.wait_ge(p0_act, evacuated(kt0_there)[1])
                    if what == "kq":
                        for c in range(C):
                            ins = pe.matmul(p0_bank(n)[:, 0:HB], wq0_sb[:, c, m * P:(m + 1) * P], kt0[:, c, :],
                                            start=(c == 0), stop=(c == C - 1))
                    if what == "bqk":
                        for c in range(C):
                            ins = pe.matmul(p0_bank(n)[0:1, 0:HB], bq0_sb[:, c:c + 1], kt0[:, c, :],
                                            start=(c == 0), stop=(c == C - 1))
                    if what == "v0":
                        ins = pe.matmul(p0_bank(n)[0:LK, 0:D], ctxT_sb[:, m * LK:(m + 1) * LK], wv0_sb[:], start=True,
                                        stop=True)
                    ins.then_inc(p0_mm, 1)

            def emptied(cut):
                for who, sem_ in (("act", p0_act), ("dve", p0_dve)):
                    pe.wait_ge(sem_, sum(BY[it[0]] == who for it in P0[:CUT[cut + 1]]))

            products(0)
            emptied(0)
            pe.wait_ge(cst_in, IN_CST)
            pe.wait_ge(set_up, 1)

            def transpose_prob(b):
                wait(pe, exp_done, b + 1)
                wait(pe, probT_copied, b)
                for u in range(U):
                    ins = pe.transpose(bank[2][0:LK, u * P:(u + 1) * P], prob[:, u * LK:(u + 1) * LK], ident[:])
                ins.then_inc(probT_done, 1)

            def attend(b):
                wait(pe, probT_copied, b + 1)
                wait(pe, x1_done, b)
                for u in range(U):
                    ins = pe.matmul(bank[3][:, u * D:(u + 1) * D], probT[:, u * P:(u + 1) * P], v0[:, cols(b, D)],
                                    start=True, stop=True)
                ins.then_inc(pv_done, 1)

            def transpose_x1(b):
                wait(pe, xq1_ready, b + 1)
                wait(pe, xT1_copied, b)
                transposes(bank[4], xq1).then_inc(xT1_done, 1)

            def gate_of(b):
                wait(pe, xT1_copied, b + 1)
                wait(pe, logit_kept, b)
                for u in range(U):
                    for c in range(C):
                        ins = pe.matmul(bank[5][:, u * P:(u + 1) * P], xT1[:, c * S + u * P:c * S + u * P + P],
                                        gate_sb[:, c, :], start=(c == 0), stop=(c == C - 1))
                ins.then_inc(logit_done, 1)

            def step(b):
                if batch(b, 1):
                    attend(b + 1)
                if batch(b, 2):
                    ahead_scores(b + 2)
                if batch(b, 0):
                    gate_of(b)
                if batch(b, 3):
                    ahead_xT(b + 3)
                if batch(b, 2):
                    transpose_prob(b + 2)
                if batch(b, 1):
                    transpose_x1(b + 1)

            step(-4)
            step(-3)
            for b in range(-2, 1):
                if b == 0:
                    pe.wait_ge(gate_in, 32)
                if b + 2 > 0:
                    emptied(b + 2)
                step(b)
                products(b + 3)
            emptied(3)
            with pe.Fori(1, B - 4) as b:
                step(b)
            for b in range(B - 4, B):
                step(b)

            pe.wait_ge(con_in, IN_CON)
            pe.wait_ge(logit_kept, B)
            def products1(lo, hi):
                for n, (what, m, h) in list(enumerate(P1, len(P0)))[lo:hi]:
                    if n >= len(P0) + 4:
                        free_bank(n)
                    if what == "kt1":
                        ins = pe.matmul(p0_bank(n)[:, 0:HB], wk1_sb[:, m * P:(m + 1) * P], ctxT_sb[:, h * HB:(h + 1) * HB],
                                        start=True, stop=True)
                    else:
                        pe.matmul(p0_bank(n)[0:LK, 0:D], ctxT_sb[:, m * LK:(m + 1) * LK], wv1_sb[:], start=True, stop=False)
                        ins = pe.matmul(p0_bank(n)[0:LK, 0:D], ones[0:1, 0:LK], bv1_sb[0:1, :], start=False, stop=True)
                    ins.then_inc(p0_mm, 1)

            products1(0, 4)
            pe.wait_ge(pairs_ok, 1)
            pm = pairs[:].rearrange("p t e -> p (t e)")
            pe.matmul(bank[0][:, 0:P], tri[:, 0:P], pm, start=True, stop=True)
            pe.matmul(bank[0][:, P:2 * P], tri[:, P:2 * P], pm, start=True, stop=True).then_inc(rank_done, 1)
            products1(4, len(P1))
            pe.wait_ge(tok_ok, 1)
            for n in range(4):
                pe.wait_ge(onerow_ok, n + 1)
                for m in range(8):
                    ins = pe.matmul(bank[1][:, 0:BLOCKS], onerow[:, n % 2, m, :], tokcol[:, 8 * n + m, :],
                                    start=(n == m == 0), stop=(n == 3 and m == 7))
                ins.then_inc(onerow_used if n < 3 else slots_done, 1)
            pe.wait_ge(split_l, CHUNKS)
            pe.wait_ge(blocks_kept, 1)
            pe.wait_ge(slots_kept, 1)
            pe.wait_ge(p0_act, 18)

            def experts(i):
                e = pe.value_load(blk_i[0:1, cols(i, 1)], min_val=0, max_val=E_FFN ** 4 - 1)
                return [e // E_FFN ** k % E_FFN * WE for k in range(4)]

            def xT_of(i, k):
                wait(pe, gathered[k], 16 * (i + 1))
                wait(pe, xl_ok, 2 * i + k - 1)
                for c in range(C):
                    ins = pe.transpose(bank[k][:, c * P:(c + 1) * P], xg[:, k, c * P:(c + 1) * P], ident[:])
                ins.then_inc(xgT_done, 1)

            def three(dst, ah, al, w, n, first, last):
                pe.matmul(dst, ah, wh[:, bass.ds(w, n)], start=first, stop=False)
                pe.matmul(dst, ah, wl[:, bass.ds(w, n)], start=False, stop=False)
                return pe.matmul(dst, al, wh[:, bass.ds(w, n)], start=False, stop=last)

            def h_of(i, k, e):
                wait(pe, xl_ok, 2 * i + k + 1)
                wait(pe, gate_ok, 2 * i + k - 1)
                for c in range(C):
                    ins = three(bank[2 + k][:], xh[:, k, c * P:(c + 1) * P], xl[:, k, c * P:(c + 1) * P], e + c * FF, FF,
                                c == 0, c == C - 1)
                ins.then_inc(h_done, 1)

            def gT_of(i, k):
                wait(pe, gate_ok, 2 * i + k + 1)
                wait(pe, gl_ok, 2 * i + k - 1)
                for c in range(FC):
                    ins = pe.transpose(bank[4 + k][:, c * P:(c + 1) * P], gate[:, k, c * P:(c + 1) * P], ident[:])
                ins.then_inc(g_done, 1)

            def y_of(i, k, e):
                wait(pe, gl_ok, 2 * i + k + 1)
                wait(pe, y_kept, 2 * i + k - 1)
                for c in range(FC):
                    ins = three(bank[6 + k][:, 0:D], gh[:, k, c * P:(c + 1) * P], gl[:, k, c * P:(c + 1) * P],
                                e + (C * FF + c * D), D, c == 0, c == FC - 1)
                ins.then_inc(y_done, 1)

            def pair(i, left=BLOCKS):
                e = experts(i)
                for k in range(2):
                    y_of(i, k, e[k])
                    if left > k + 1:
                        gT_of(*ahead_of(i, k, 1))
                    if left > k + 2:
                        h_of(*ahead_of(i, k, 2), e[k + 2])
                    if left > k + 3:
                        xT_of(*ahead_of(i, k, 3))

            xT_of(0, 0)
            xT_of(0, 1)
            e = experts(0)
            h_of(0, 0, e[0])
            gT_of(0, 0)
            h_of(0, 1, e[1])
            xT_of(1, 0)
            pair(0)
            with pe.Fori(1, BLOCKS // 2 - 2) as i:
                pair(i)
            pair(BLOCKS // 2 - 2, 4)
            pair(BLOCKS // 2 - 1, 2)

            def transpose_p(b, u, j):
                wait(pe, e_ok, 8 * b + 4 * u + j + 1)
                wait(pe, pT_ok, 8 * b + 4 * u + j - 1)
                for n in range(HG):
                    ins = pe.transpose(bank[4 + j % 2][0:LK, n * P:(n + 1) * P], sc[:, j, n * LK:(n + 1) * LK], ident[:])
                ins.then_inc(t_done, 1)

            def values(b, u, j):
                wait(pe, pT_ok, 8 * b + 4 * u + j + 1)
                if j == 0:
                    wait(pe, ot_ok, 2 * b + u)
                    wait(pe, v_ok, b + 1)
                for n, (c, _, h) in enumerate(heads_of(j)):
                    ins = pe.matmul(bank[6][:, c * P:(c + 1) * P], vnow[:, h, :], pT[:, j, n * P:(n + 1) * P],
                                    start=(j == n == 0), stop=(j == NB - 1 and n % 2 == 1), skip_group_check=True)
                ins.then_inc(pvj_done, 1)

            def transpose_x(b, u):
                wait(pe, xn2_ok, 2 * b + u + 1)
                wait(pe, recT_ok, 2 * b + u - 2)
                wait(pe, ql_ok, 2 * b + u)
                for c in range(C):
                    ins = pe.transpose(bank[7][:, c * P:(c + 1) * P], xq2[:, u, c * P:(c + 1) * P], ident[:])
                ins.then_inc(xt_done, 1)

            def queries(b, u):
                wait(pe, xt_ok, 2 * b + u + 1)
                for m in range(C):
                    for c in range(C):
                        ins = pe.matmul(bank[7][:, m * P:(m + 1) * P], wq1_sb[:, c, m * P:(m + 1) * P],
                                        xT2[:, c * P:(c + 1) * P], start=(c == 0), stop=(c == C - 1))
                ins.then_inc(q_done, 1)

            def scores(b, u, j):
                if j == 0:
                    wait(pe, ql_ok, 2 * b + u + 1)
                    wait(pe, know_ok, b + 1)
                wait(pe, e_ok, 8 * b + 4 * u + j - 3)
                g = slice(32 * j, 32 * j + 32)
                for c in range(C):
                    for n, (q, part) in enumerate(((qh, 0), (qh, 1), (ql, 0))):
                        ins = pe.matmul(bank[j][:, c * 2 * LK:(c + 1) * 2 * LK], q[g, u, c * P:(c + 1) * P],
                                        know[g, part * C + c].rearrange("p k n -> p (k n)"), start=(n == 0), stop=(n == 2))
                ins.then_inc(s_done, 1)

            def transpose_rec(b, u):
                wait(pe, rec_ok, 2 * b + u + 1)
                wait(pe, x3_ok, 2 * b + u)
                wait(pe, ql_ok, 2 * b + u + 3 if has(b, u, 2) else TILES)
                for c in range(C):
                    ins = pe.transpose(bank[7][:, c * P:(c + 1) * P],
                                       rec[:, c * P // DK:(c + 1) * P // DK, :].rearrange("p h d -> p (h d)"), ident[:])
                ins.then_inc(r_done, 1)

            def project(b, u):
                wait(pe, ot_ok, 2 * b + u + 1)
                wait(pe, ql_ok, 2 * b + u + 4 if has(b, u, 3) else TILES)
                wait(pe, recT_ok, 2 * b + u + 1)
                for c in range(C):
                    ins = pe.matmul(bank[7][:, 0:D], oT[:, c * P:(c + 1) * P], wo1_sb[:, c, :],
                                    start=(c == 0), stop=(c == C - 1))
                ins.then_inc(wo_done, 1)

            def slot(b, u):
                if has(b, u, 0):
                    transpose_p(b, u, 0)
                if has(b, u, 2):
                    transpose_x(*ahead_of(b, u, 2))
                if has(b, u, 0):
                    transpose_p(b, u, 1)
                if has(b, u, 2):
                    queries(*ahead_of(b, u, 2))
                if has(b, u, 0):
                    values(b, u, 0)
                    transpose_p(b, u, 2)
                    values(b, u, 1)
                    transpose_p(b, u, 3)
                if has(b, u, -1):
                    project(*ahead_of(b, u, -1))
                if has(b, u, 1):
                    scores(*ahead_of(b, u, 1), 0)
                if has(b, u, 0):
                    transpose_rec(b, u)
                if has(b, u, 1):
                    scores(*ahead_of(b, u, 1), 1)
                if has(b, u, 0):
                    values(b, u, 2)
                if has(b, u, 1):
                    scores(*ahead_of(b, u, 1), 2)
                    scores(*ahead_of(b, u, 1), 3)
                if has(b, u, 0):
                    values(b, u, 3)

            def whole_peak(c, n):
                pe.wait_ge(red_ok, n)
                pe.transpose(bank[0][0:1, 0:P], red[:, c:c + 1], ident[:]).then_inc(red_done, 1)
                pe.wait_ge(peak_ok, n)
                pe.matmul(bank[1][:, 0:1], ones[0:1, :], peak[0:1, c:c + 1], start=True, stop=True).then_inc(peak_done, 1)

            whole_peak(1, 1)
            pe.wait_ge(l1_in, 16 * 6)
            pe.wait_ge(y_kept, BLOCKS)
            def pair(i):
                slot(i, 0)
                slot(i, 1)

            slot(-2, 1)
            pair(-1)
            pair(0)
            with pe.Fori(1, B - 2) as i:
                pair(i)
            pair(B - 2)
            pair(B - 1)
            slot(B, 0)

            whole_peak(0, 2)
            pe.wait_ge(wf8_ok, 1)

            def linear(b, k):
                wait(pe, y8_ok, b + 1)
                wait(pe, y8T_ok, b)
                dst = bank[2][:].bitcast(BF16)
                for c in range(C):
                    for u in range(U):
                        ins = pe.transpose(dst[:, c * S + u * P:c * S + u * P + P],
                                           y8[:, u * D + c * P:u * D + c * P + P], identb[:])
                ins.then_inc(y8_done, 1)
                wait(pe, y8T_ok, b + 1)
                wait(pe, zf_ok, b - 1)
                for u in range(U):
                    for c in range(C):
                        ins = pe.matmul(bank[4 + k][:, u * D:(u + 1) * D], y8T[:, c * S + u * P:c * S + u * P + P],
                                        wf8[:, c * D:(c + 1) * D], start=(c == 0), stop=(c == C - 1))
                ins.then_inc(acc_done, 1)

            linear(0, 0)
            linear(1, 1)
            with pe.Fori(1, B // 2) as i:
                for k in range(2):
                    linear(2 * i + k, k)


def kernel(**inputs):
    import concourse.bacc as bacc
    import ml_dtypes
    from concourse.bass_utils import run_bass_kernel_spmd

    a = {k: np.asarray(v) for k, v in inputs.items()}

    def chunked(w):
        return w.reshape(-1, P, w.shape[-1]).transpose(1, 0, 2)

    w1 = a["L0_ffn_w1"].transpose(0, 2, 1).reshape(E_FFN, C, P, FF).transpose(2, 0, 1, 3).reshape(P, E_FFN, C * FF)
    w2 = a["L0_ffn_w2"].transpose(0, 2, 1).reshape(E_FFN, FC, P, D).transpose(2, 0, 1, 3).reshape(P, E_FFN, FC * D)
    p, t = np.arange(P)[:, None], np.arange(2 * TILES)[None, :] % TILES
    tri = np.concatenate([np.triu(np.ones((P, P)), 1), np.ones((P, P))], axis=1)
    arrays = dict(
        x=a["x"].reshape(B * S, D), ctxT=a["ctx_512"].transpose(2, 0, 1).reshape(-1, B * LK),
        wq0T=chunked(a["L0_xattn_Wq"].T), wk0=a["L0_xattn_Wk"], wv0=a["L0_xattn_Wv"],
        bq0=a["L0_xattn_bq"].reshape(C, P).T, bk0=a["L0_xattn_bk"].reshape(C, P).T, bv0=a["L0_xattn_bv"],
        gateT=chunked(a["L0_ffn_gate_w"].T), gbias=np.tile(a["L0_ffn_expert_bias"], U),
        wmoe=np.concatenate([w1, w2], axis=2).reshape(P, -1),
        wq1=chunked(a["L1_xattn_Wq"]), wk1=a["L1_xattn_Wk"], wv1=a["L1_xattn_Wv"], wo1=chunked(a["L1_xattn_Wo"]),
        bq1=a["L1_xattn_bq"].reshape(C, P).T, bk1=a["L1_xattn_bk"].reshape(C, P).T, bv1=a["L1_xattn_bv"].reshape(1, D),
        bo1=a["L1_xattn_bo"], wfT=chunked(a["L1_ffn_weight"].T).reshape(P, C * D), bf=a["L1_ffn_bias"],
        gains=np.stack([a["g_xattn"], a["g_ffn"]], axis=1).reshape(-1),
        c_ident=np.eye(P, dtype=np.float32), c_tri=tri.astype(ml_dtypes.bfloat16),
        c_count=np.tile(np.arange(P, dtype=np.float32), (P, 1)),
        c_token=(t // U * S + U * p + t % U).astype(np.float32),
        c_head=np.stack([(p[:, 0] // DK % 2 == 0) * 0.25, (p[:, 0] // DK % 2 == 1) * 0.25], axis=1).astype(np.float32),
    )
    nc = bacc.Bacc("TRN2", target_bir_lowering=False, num_devices=1)
    args = {}
    for name in arrays:
        arrays[name] = np.ascontiguousarray(arrays[name])
        args[name] = nc.dram_tensor(f"in_{name}", arrays[name].shape, mybir.dt.from_np(arrays[name].dtype),
                                    kind="ExternalInput").ap()
    out = nc.dram_tensor("out_x", (B * S, D), F32, kind="ExternalOutput").ap()
    build(nc, out=out, **args)
    r = run_bass_kernel_spmd(nc, [{f"in_{k}": v for k, v in arrays.items()}], core_ids=[0])
    return r.results[0]["out_x"].reshape(B, S, D)
```
